# Optimizing a Trainium2 kernel written in Bass

```python
import numpy as np
import jax
import jax.numpy as jnp

def _softmax(x, axis=-1):
    return jax.nn.softmax(x, axis=axis)

def _gelu(x):
    return jax.nn.gelu(x, approximate=True)

def _silu(x):
    return jax.nn.silu(x)

def _sigmoid(x):
    return jax.nn.sigmoid(x)

def _layernorm(x, axis=-1, eps=1e-05):
    m = jnp.mean(x, axis=axis, keepdims=True)
    v = jnp.var(x, axis=axis, keepdims=True)
    return (x - m) / jnp.sqrt(v + eps)

def _scatter_add(tgt, idx, src, axis=0):
    return tgt.at[idx].add(src)

def _segment_sum(src, seg, n):
    return jax.ops.segment_sum(src, seg, n)
kernel_name = 'mk_sandwich_d1_jaxref_r8_4865eb'

def setup_inputs(seed: int=0):
    np.random.seed(seed)
    _w = jnp.asarray

    def _L0_attn_setup():
        import jax, jax.numpy as jnp
        import numpy as np
        B, S, E, H = (2, 256, 128, 16)
        D = E // H
        key = jax.random.key(seed)
        k1, k2, k3 = jax.random.split(key, 3)
        x = jax.random.normal(k1, (B, S, E), dtype=jnp.float32)
        lim_qkv = np.sqrt(6.0 / (E + 3 * E)).astype(np.float32)
        lim_out = np.sqrt(6.0 / (E + E)).astype(np.float32)
        w_qkv = jax.random.uniform(k2, (E, 3 * E), jnp.float32, -lim_qkv, lim_qkv)
        w_out = jax.random.uniform(k3, (E, E), jnp.float32, -lim_out, lim_out)
        return {'x': x, 'w_qkv': w_qkv, 'w_out': w_out}
    _L0_attn_in = _L0_attn_setup()

    def _L0_ffn_setup():
        import jax, jax.numpy as jnp
        import numpy as np
        QK_SCALE = 10.0
        NEG_INF = -1000000000.0

        def layernorm(x, g, b, eps=1e-05):
            mu = jnp.mean(x, axis=-1, keepdims=True)
            var = jnp.var(x, axis=-1, keepdims=True)
            return (x - mu) * jax.lax.rsqrt(var + eps) * g + b

        def l2norm(x, eps=1e-12):
            return x / jnp.sqrt(jnp.sum(x * x, axis=-1, keepdims=True) + eps)
        key = jax.random.key(seed)
        ks = jax.random.split(key, 10)
        B, S, D, H, DH, E, FF = (2, 128, 128, 16, 64, 8, 512)
        sd = lambda fan: 1.0 / np.sqrt(fan)
        return {'x': jax.random.normal(ks[0], (B, S, D), jnp.float32), 'ln_g': jnp.ones((D,), jnp.float32), 'ln_b': jnp.zeros((D,), jnp.float32), 'Wq': jax.random.normal(ks[1], (D, H * DH), jnp.float32) * sd(D), 'Wk': jax.random.normal(ks[2], (D, H * DH), jnp.float32) * sd(D), 'Wv': jax.random.normal(ks[3], (D, H * DH), jnp.float32) * sd(D), 'q_scale': jnp.ones((H, 1, DH), jnp.float32), 'k_scale': jnp.ones((H, 1, DH), jnp.float32), 'Wo': jax.random.normal(ks[4], (H * DH, D), jnp.float32) * sd(H * DH), 'gate_w': jax.random.normal(ks[5], (D, E), jnp.float32) * sd(D), 'gate_b': jnp.zeros((E,), jnp.float32), 'w1': jax.random.normal(ks[6], (E, D, FF), jnp.float32) * sd(D), 'b1': jnp.zeros((E, FF), jnp.float32), 'w2': jax.random.normal(ks[7], (E, FF, D), jnp.float32) * sd(FF), 'b2': jnp.zeros((E, D), jnp.float32)}
    _L0_ffn_in = _L0_ffn_setup()
    _d = {'L0_attn_x': _L0_attn_in['x'], 'L0_attn_w_qkv': _L0_attn_in['w_qkv'], 'L0_attn_w_out': _L0_attn_in['w_out'], 'L0_ffn_ln_g': _L0_ffn_in['ln_g'], 'L0_ffn_ln_b': _L0_ffn_in['ln_b'], 'L0_ffn_Wq': _L0_ffn_in['Wq'], 'L0_ffn_Wk': _L0_ffn_in['Wk'], 'L0_ffn_Wv': _L0_ffn_in['Wv'], 'L0_ffn_q_scale': _L0_ffn_in['q_scale'], 'L0_ffn_k_scale': _L0_ffn_in['k_scale'], 'L0_ffn_Wo': _L0_ffn_in['Wo'], 'L0_ffn_gate_w': _L0_ffn_in['gate_w'], 'L0_ffn_gate_b': _L0_ffn_in['gate_b'], 'L0_ffn_w1': _L0_ffn_in['w1'], 'L0_ffn_b1': _L0_ffn_in['b1'], 'L0_ffn_w2': _L0_ffn_in['w2'], 'L0_ffn_b2': _L0_ffn_in['b2']}
    _x0 = _d['L0_attn_x']
    _d['L0_attn_x'] = jax.random.normal(jax.random.fold_in(jax.random.key(seed), 1), (16, 256, 128), dtype=_x0.dtype)
    del _x0
    return _d

def reference(L0_attn_x, L0_attn_w_qkv, L0_attn_w_out, L0_ffn_ln_g, L0_ffn_ln_b, L0_ffn_Wq, L0_ffn_Wk, L0_ffn_Wv, L0_ffn_q_scale, L0_ffn_k_scale, L0_ffn_Wo, L0_ffn_gate_w, L0_ffn_gate_b, L0_ffn_w1, L0_ffn_b1, L0_ffn_w2, L0_ffn_b2):

    def _L0_attn_ref(x, w_qkv, w_out):
        import jax, jax.numpy as jnp
        import numpy as np
        B, S, E, H = (2, 256, 128, 16)
        D = E // H
        b, s, e = x.shape
        qkv = jnp.einsum('bse,ef->bsf', x, w_qkv)
        qkv = qkv.reshape(b, s, 3, H, D).transpose(2, 0, 3, 1, 4)
        q, k, v = (qkv[0], qkv[1], qkv[2])
        scale = 1.0 / np.sqrt(D).astype(np.float32)
        scores = jnp.einsum('bhsd,bhtd->bhst', q, k) * scale
        attn = jax.nn.softmax(scores, axis=-1)
        out = jnp.einsum('bhst,bhtd->bhsd', attn, v)
        out = out.transpose(0, 2, 1, 3).reshape(b, s, e)
        return jnp.einsum('bse,ef->bsf', out, w_out)

    def _L0_ffn_ref(x, ln_g, ln_b, Wq, Wk, Wv, q_scale, k_scale, Wo, gate_w, gate_b, w1, b1, w2, b2):
        import jax, jax.numpy as jnp
        import numpy as np
        QK_SCALE = 10.0
        NEG_INF = -1000000000.0

        def layernorm(x, g, b, eps=1e-05):
            mu = jnp.mean(x, axis=-1, keepdims=True)
            var = jnp.var(x, axis=-1, keepdims=True)
            return (x - mu) * jax.lax.rsqrt(var + eps) * g + b

        def l2norm(x, eps=1e-12):
            return x / jnp.sqrt(jnp.sum(x * x, axis=-1, keepdims=True) + eps)
        B, S, D = x.shape
        H = q_scale.shape[0]
        DH = q_scale.shape[-1]
        h = layernorm(x, ln_g, ln_b)
        q = (h @ Wq).reshape(B, S, H, DH).transpose(0, 2, 1, 3)
        k = (h @ Wk).reshape(B, S, H, DH).transpose(0, 2, 1, 3)
        v = (h @ Wv).reshape(B, S, H, DH).transpose(0, 2, 1, 3)
        q = l2norm(q) * q_scale
        k = l2norm(k) * k_scale
        logits = jnp.einsum('bhid,bhjd->bhij', q, k) * QK_SCALE
        causal = jnp.tril(jnp.ones((S, S), bool))
        logits = jnp.where(causal, logits, NEG_INF)
        attn = jax.nn.softmax(logits, axis=-1)
        out = jnp.einsum('bhij,bhjd->bhid', attn, v)
        out = out.transpose(0, 2, 1, 3).reshape(B, S, H * DH) @ Wo
        h = layernorm(out, ln_g, ln_b)
        gate = jax.nn.softmax(h @ gate_w + gate_b, axis=-1)
        hid = jax.nn.gelu(jnp.einsum('bsd,edf->bsef', h, w1) + b1)
        exp_out = jnp.einsum('bsef,efd->bsed', hid, w2) + b2
        moe = jnp.einsum('bse,bsed->bsd', gate, exp_out)
        return layernorm(moe, ln_g, ln_b)
    x = L0_attn_x
    x = x + _layernorm(_L0_attn_ref(_layernorm(x, axis=-1), L0_attn_w_qkv, L0_attn_w_out), axis=-1)
    x = x + _layernorm(_L0_ffn_ref(_layernorm(x, axis=-1), L0_ffn_ln_g, L0_ffn_ln_b, L0_ffn_Wq, L0_ffn_Wk, L0_ffn_Wv, L0_ffn_q_scale, L0_ffn_k_scale, L0_ffn_Wo, L0_ffn_gate_w, L0_ffn_gate_b, L0_ffn_w1, L0_ffn_b1, L0_ffn_w2, L0_ffn_b2), axis=-1)
    return x

_drawn_inputs = setup_inputs


def setup_inputs(seed=0):
    import zlib

    import numpy as np

    out = dict(_drawn_inputs(seed))
    spreads = {'L0_ffn_ln_g': (1.0, 0.2),
     'L0_ffn_ln_b': (0.0, 0.1),
     'L0_ffn_q_scale': (1.0, 0.2),
     'L0_ffn_k_scale': (1.0, 0.2),
     'L0_ffn_gate_b': (0.0, 0.1),
     'L0_ffn_b1': (0.0, 0.1),
     'L0_ffn_b2': (0.0, 0.1)}
    factors = {}
    for name, (base, spread) in spreads.items():
        noise = np.random.default_rng([zlib.crc32(name.encode()), seed]).standard_normal(out[name].shape)
        drawn = base * np.exp(spread * noise) if base else spread * noise
        out[name] = jnp.asarray(drawn.astype(out[name].dtype))
    for name, factor in factors.items():
        out[name] = (out[name] * factor).astype(out[name].dtype)
    return out
```

```python
from contextlib import ExitStack

import concourse.bass as bass
from concourse import mybir

F32 = mybir.dt.float32
I32 = mybir.dt.int32
ALU = mybir.AluOpType
ACT = mybir.ActivationFunctionType
X_AXIS = mybir.AxisListType.X

P = 128
LN_EPS = 1e-5
L2_EPS = 1e-12
QK_SCALE = 10.0
MASKED = -1.0e30
RSQRT_MAGIC = float(0x5F3759DF)
NORM_LINKS = 14


def ds(start, size):
    return bass.ds(start, size)


class Link:

    def __init__(self, engine, sem, base):
        self.engine, self.sem, self.base, self.n = engine, sem, base, 0

    def __call__(self, instruction):
        self.n += 1
        instruction.then_inc(self.sem, 1)
        self.engine.wait_ge(self.sem, self.base + self.n)


def sandwich_kernel(nc, x, w_qkv, w_out, ln_g, ln_b, Wq, Wk, Wv, q_scale, k_scale, Wo, gate_w, gate_b,
                    w1, b1, w2, b2, out):
    NB, S, E = x.shape
    ST = S // P
    NT = NB * ST
    H1 = 16
    D1 = E // H1
    H2, _, D2 = q_scale.shape
    NP = H2 * D2 // P
    NE, _, FF = w1.shape
    FC = FF // P
    assert E == P and ST == 2 and D2 * 2 == P and H2 == 2 * NP
    CT = 4
    NCH = NT // CT
    CW = CT * P

    ctx = ExitStack()
    with ctx:
        def sb(name, shape, dt=F32):
            return ctx.enter_context(nc.sbuf_tensor(name, shape, dt))

        def sem(name):
            return ctx.enter_context(nc.semaphore(name))

        bank = [ctx.enter_context(nc.psum_tensor(f"bank{i}", [P, 512], F32)) for i in range(8)]

        xres = sb("xres", [P, NT * P])
        hTres = sb("hTres", [P, NT * P])
        moe0 = sb("moe0", [P, NT * P])
        gates = sb("gates", [P, NT * NE])
        wqkv_sb = sb("wqkv_sb", [P, 3 * E])
        wout_sb = sb("wout_sb", [P, E])
        wq_sb = sb("wq_sb", [P, H2 * D2])
        wk_sb = sb("wk_sb", [P, H2 * D2])
        wv_sb = sb("wv_sb", [P, H2 * D2])
        wo_sb = sb("wo_sb", [P, NP, E])
        gw_sb = sb("gw_sb", [P, NE])
        w1_sb = sb("w1_sb", [P, NE, FF])
        w2_sb = sb("w2_sb", [P, NE * FC, E])
        b2_sb = sb("b2_sb", [NE, E])
        R_B1, R_QS, R_KS, R_G, R_B, R_GB = 0, NE * FC, NE * FC + NP, NE * FC + 2 * NP, NE * FC + 2 * NP + 1, NE * FC + 2 * NP + 2
        vrows = sb("vrows", [P, P])
        vcols = sb("vcols", [P, P])
        qks = sb("qks", [P, NP])
        gspread = sb("gspread", [P, 3, P])
        gnat = sb("gnat", [P, 2, P])
        gbnat = sb("gbnat", [P, NE])
        ident = sb("ident", [P, P])
        headmask = sb("headmask", [P, H1])
        causal = sb("causal", [P, 2, P])
        blockones = sb("blockones", [P, P])
        eps12 = sb("eps12", [P, 1])

        bst = sb("bst", [P, CT, 6])
        mv = sb("mv", [P, CT, 2])
        pad = sb("pad", [P, 64])
        rs_v = sb("rs_v", [P, CT])
        rs_t = sb("rs_t", [P, CT], I32)
        rs_i = sb("rs_i", [P, CT], I32)
        rs_a = sb("rs_a", [P, CT])
        rs_y = sb("rs_y", [P, CT])

        xh = sb("xh", [P, ST, P])
        xT = sb("xT", [P, S])
        qT = sb("qT", [P, S])
        kT = sb("kT", [P, S])
        kz = sb("kz", [P, H1, S])
        vaug = sb("vaug", [P, ST, H1, D1 + 1])
        nmax = sb("nmax", [P, 4, ST])
        prob = sb("prob", [P, 3, ST, S])
        probT = sb("probT", [P, 2, ST, S])
        rsum = sb("rsum", [P, ST, H1])
        onat = sb("onat", [P, ST, P])
        oT = sb("oT", [P, S])
        tmp = sb("tmp", [P, CT, P])

        hT = sb("hT", [P, S])
        qTs = sb("qTs", [P, 2, S])
        sq = sb("sq", [P, 2, S])
        rk = sb("rk", [P, S])
        lq = sb("lq", [P, 4])
        rq = sb("rq", [P, 4])
        nrq = sb("nrq", [P, 2, ST, 2])
        kpair = sb("kpair", [P, 2, 2, S])
        vpair = sb("vpair", [P, 4, ST, 2, D2 + 1])
        smask = sb("smask", [P, 4, 3 * P])
        nmax2 = sb("nmax2", [P, 4, ST])
        prob2 = sb("prob2", [P, 4, 3 * P])
        prob2T = sb("prob2T", [P, 2, 3 * P])
        rsum2 = sb("rsum2", [P, ST, 2])
        onat2 = sb("onat2", [P, ST, P])
        oT2 = sb("oT2", [P, NP, S])
        h2n = sb("h2n", [P, ST, P])
        h2T = sb("h2T", [P, S])
        glog = sb("glog", [P, ST, NE])
        gmx = sb("gmx", [P, ST])
        gsm = sb("gsm", [P, ST])
        gnorm = sb("gnorm", [P, ST, NE])
        gT = sb("gT", [NE, S])

        hid = sb("hid", [P, 2, FC, CW])
        acc = sb("acc", [P, CT, P])
        gch = sb("gch", [P, CT, NE])
        fin = sb("fin", [P, 2, CT, P])

        s_x, s_wa, s_wb, s_wc, s_vec, s_out = (sem(n) for n in ("s_x", "s_wa", "s_wb", "s_wc", "s_vec", "s_out"))
        s_vz, s_const, s_zero, s_vcol_ps, s_vcols, s_spread, s_nat_ps, s_nat = (
            sem(n) for n in ("s_vz", "s_const", "s_zero", "s_vcol_ps", "s_vcols", "s_spread", "s_nat_ps", "s_nat"))
        s_cst1 = sem("s_cst1")
        s_link = sem("s_link")
        a_xh, a_xT_ps, a_xT, a_qk_ps, a_v_ps, a_qT, a_kT, a_kz, a_v = (
            sem("a_" + n) for n in ("xh", "xT_ps", "xT", "qk_ps", "v_ps", "qT", "kT", "kz", "v"))
        a_s, a_nmax, a_exp, a_t, a_pT, a_pv, a_onat, a_oT_ps, a_oT, a_y, a_ydone, a_link = (
            sem("a_" + n) for n in ("s", "nmax", "exp", "t", "pT", "pv", "onat", "oT_ps", "oT", "y", "ydone", "link"))
        b_xh, b_hT_ps, b_hT, b_qk_ps, b_sq, b_q, b_kn_ps, b_rk, b_lq, b_rq, b_nrq, b_k, b_v_ps, b_v = (
            sem("b_" + n) for n in ("xh", "hT_ps", "hT", "qk_ps", "sq", "q", "kn_ps", "rk", "lq", "rq", "nrq", "k", "v_ps", "v"))
        b_s, b_m, b_exp, b_t, b_pT, b_pv, b_onat, b_oT_ps, b_oT, b_y, b_link, b_l1 = (
            sem("b_" + n) for n in ("s", "m", "exp", "t", "pT", "pv", "onat", "oT_ps", "oT", "y", "link", "l1"))
        b_h2n, b_h2T_ps, b_h2T, b_gl, b_glog, b_gexp, b_gate, b_gT_ps, b_gT, b_gb, b_gbs, b_res = (
            sem("b_" + n) for n in ("h2n", "h2T_ps", "h2T", "gl", "glog", "gexp", "gate", "gT_ps", "gT", "gb", "gbs", "res"))
        c_h, c_hid, c_e, c_acc, c_link, c_fin = (sem("c_" + n) for n in ("h", "hid", "e", "acc", "link", "fin"))

        block = ctx.enter_context(nc.Block())

        XQ = 4
        x_rows = x.rearrange("b (i p) e -> p (b i) e", p=P)
        out_rows = out.rearrange("b (i p) e -> p (b i) e", p=P)
        xres_t = xres[:, :].rearrange("p (t e) -> p t e", e=P)

        @block.sync
        def _(sp):
            sp.wait_ge(s_vz, 1)
            n = NT // XQ
            sp.dma_start(xres_t[:, 0:n, :], x_rows[:, 0:n, :]).then_inc(s_x, 16)
            sp.dma_start(wqkv_sb[:, :], w_qkv).then_inc(s_wa, 16)
            sp.dma_start(wout_sb[:, :], w_out).then_inc(s_wa, 16)
            for i in range(1, XQ):
                sp.dma_start(xres_t[:, i * n:(i + 1) * n, :], x_rows[:, i * n:(i + 1) * n, :]).then_inc(s_x, 16)
            sp.dma_start(vrows[R_B1:R_B1 + NE * FC, :], b1.rearrange("e (c f) -> (e c) f", f=P)).then_inc(s_vec, 16)
            sp.dma_start(vrows[R_QS:R_QS + NP, :], q_scale.rearrange("(p t) o d -> p (t o d)", t=2)).then_inc(s_vec, 16)
            sp.dma_start(vrows[R_KS:R_KS + NP, :], k_scale.rearrange("(p t) o d -> p (t o d)", t=2)).then_inc(s_vec, 16)
            sp.dma_start(vrows[R_G:R_G + 1, :], ln_g.rearrange("(a d) -> a d", a=1)).then_inc(s_vec, 16)
            sp.dma_start(vrows[R_B:R_B + 1, :], ln_b.rearrange("(a d) -> a d", a=1)).then_inc(s_vec, 16)
            sp.dma_start(vrows[R_GB:R_GB + 1, 0:NE], gate_b.rearrange("(a d) -> a d", a=1)).then_inc(s_vec, 16)
            for w_sb, w in ((wq_sb, Wq), (wk_sb, Wk), (wv_sb, Wv), (gw_sb, gate_w), (b2_sb, b2)):
                sp.dma_start(w_sb[:, :], w).then_inc(s_wb, 16)
            sp.dma_start(wo_sb[:, :, :], Wo.rearrange("(k p) e -> p k e", p=P)).then_inc(s_wb, 16)
            sp.dma_start(w1_sb[:, :, :], w1.rearrange("e d f -> d e f")).then_inc(s_wc, 16)
            sp.dma_start(w2_sb[:, :, :], w2.rearrange("e (c f) d -> f (e c) d", f=P)).then_inc(s_wc, 16)
            with sp.Fori(0, NCH // 2) as ii:
                for j in range(2):
                    sp.wait_ge(c_fin, ii * 2 + (j + 1))
                    sp.dma_start(out_rows[:, ds(ii * (2 * CT) + j * CT, CT), :], fin[:, j, :, :]).then_inc(s_out, 16)
            sp.wait_ge(s_out, 16 * NCH)

        @block.gpsimd
        def _(pool):
            nc.gpsimd.memset(vrows[:, :], 0.0).then_inc(s_vz, 1)
            nc.gpsimd.memset(ident[:, :], 0.0).then_inc(s_cst1, 1)
            nc.gpsimd.memset(headmask[:, :], 1.0).then_inc(s_cst1, 1)
            nc.gpsimd.memset(causal[:, :, :], 0.0).then_inc(s_cst1, 1)
            nc.gpsimd.memset(eps12[:, :], L2_EPS).then_inc(s_const, 1)
            pool.wait_ge(s_cst1, 3)
            nc.gpsimd.affine_select(out=ident[:, :], in_=ident[:, :], compare_op=ALU.not_equal, fill=1.0,
                                    base=0, pattern=[[-1, P]], channel_multiplier=1).then_inc(s_const, 1)
            nc.gpsimd.affine_select(out=headmask[:, :], in_=headmask[:, :], compare_op=ALU.is_ge, fill=0.0,
                                    base=0, pattern=[[-D1, H1]], channel_multiplier=1).then_inc(s_cst1, 1)
            pool.wait_ge(s_cst1, 4)
            nc.gpsimd.affine_select(out=headmask[:, :], in_=headmask[:, :], compare_op=ALU.is_ge, fill=0.0,
                                    base=D1 - 1, pattern=[[D1, H1]], channel_multiplier=-1).then_inc(s_const, 1)
            nc.gpsimd.affine_select(out=causal[:, 1, :], in_=causal[:, 1, :], compare_op=ALU.is_ge, fill=MASKED,
                                    base=0, pattern=[[-1, P]], channel_multiplier=1).then_inc(s_const, 1)

            pool.wait_ge(s_const, 6)
            HG = 4

            def mask_keys(b):
                pool.wait_ge(a_kT, b + 1)
                for j in range(H1 // HG):
                    nc.gpsimd.tensor_tensor(
                        kz[:, HG * j:HG * (j + 1), :],
                        kT[:, :].unsqueeze(1).broadcast_to([P, HG, S]),
                        headmask[:, HG * j:HG * (j + 1)].unsqueeze(2).broadcast_to([P, HG, S]),
                        ALU.mult).then_inc(a_kz, 1)

            with pool.Fori(0, NB) as b:
                mask_keys(b)
            with pool.Fori(0, NB) as b:
                pool.wait_ge(b_h2T, b + 1)
                nc.gpsimd.tensor_copy(hTres[:, ds(b * S, S)], h2T[:, :]).then_inc(b_res, 1)

        carried = [0]

        def carry_wait():
            carried[0] += 1
            nc.vector.memset(pad[:, carried[0] % 64:carried[0] % 64 + 1], 0.0)

        def rsqrt_steps(link, n, var, eps):
            v, t, i, a, y = (q[:, 0:n] for q in (rs_v, rs_t, rs_i, rs_a, rs_y))
            link(nc.vector.tensor_scalar_add(v, var, eps))
            link(nc.vector.tensor_single_scalar(t, v.bitcast(I32), 1, ALU.arith_shift_right))
            link(nc.vector.tensor_scalar(i, t, -1.0, RSQRT_MAGIC, ALU.mult, ALU.add))
            guess = i.bitcast(F32)
            for step in range(3):
                yy = guess if step == 0 else y
                link(nc.vector.tensor_tensor(a, yy, yy, ALU.mult))
                link(nc.vector.scalar_tensor_tensor(a, a, -0.5, v, ALU.mult, ALU.mult))
                link(nc.vector.scalar_tensor_tensor(y, a, 1.5, yy, ALU.add, ALU.mult))

        def norm_stats(link, tiles):
            n = len(tiles)
            for i, tile in enumerate(tiles):
                last = nc.vector.bn_stats(bst[:, i, :], tile)
            link(last)
            carry_wait()
            for i in range(n):
                last = nc.vector.bn_aggr(mv[:, i, :], bst[:, i, :])
            link(last)
            rsqrt_steps(link, n, mv[:, 0:n, 1], LN_EPS)

        def normalize(dst, src, i):
            return nc.vector.tensor_scalar(dst, src, mv[:, i, 0:1], rs_y[:, i:i + 1], ALU.subtract, ALU.mult)

        SB, TB = bank[0:3], bank[3:5]
        QK, VX, OB = bank[5], bank[6], bank[7]
        O1 = OB[:, 0:ST * H1 * (D1 + 1)].rearrange("p (i h d) -> p i h d", i=ST, h=H1)
        S2, T2 = bank[0:2], bank[3:5]
        QK2, VN2, OB2, Y2 = bank[5], bank[6], bank[7], bank[2]
        O2 = OB2[:, 0:ST * 2 * (D2 + 1)].rearrange("p (i h d) -> p i h d", i=ST, h=2)
        QN2 = T2[0][:, 3 * P:3 * P + 4]
        HB, EB = bank[0:4], bank[4:6]

        BLOCKS = ((0, 0), (1, 0), (1, 1))

        @block.tensor
        def _(pe):
            pe.wait_ge(s_const, 6)
            pe.wait_ge(s_vec, 16 * 6)
            nc.tensor.transpose(bank[0][:, 0:P], vrows[:, :], ident[:, :]).then_inc(s_vcol_ps, 1)
            pe.wait_ge(s_spread, 1)
            for i in range(3):
                last = nc.tensor.transpose(bank[1][:, i * P:(i + 1) * P], gspread[:, i, :], ident[:, :])
            last.then_inc(s_nat_ps, 1)
            pe.wait_ge(s_nat, 1)
            pe.wait_ge(s_wa, 32)

            def a_turn_x(b):
                pe.wait_ge(a_xh, b + 1)
                for i in range(ST):
                    last = nc.tensor.transpose(VX[:, (ST + i) * P:(ST + i + 1) * P], xh[:, i, :], ident[:, :])
                last.then_inc(a_xT_ps, 1)

            def a_project(b):
                pe.wait_ge(a_xT, b + 1)
                nc.tensor.matmul(QK[:, 0:S], wqkv_sb[:, 0:E], xT[:, :], start=True, stop=True)
                nc.tensor.matmul(QK[:, S:2 * S], wqkv_sb[:, E:2 * E], xT[:, :], start=True, stop=True).then_inc(a_qk_ps, 1)
                for i in range(ST):
                    last = nc.tensor.matmul(VX[:, i * P:(i + 1) * P], xT[:, i * P:(i + 1) * P],
                                            wqkv_sb[:, 2 * E:3 * E], start=True, stop=True)
                last.then_inc(a_v_ps, 1)

            def a_batch(b, last_batch):
                pe.wait_ge(a_qT, b + 1)
                for k in range(H1 + 3):
                    if k < H1:
                        if k % 4 == 0:
                            pe.wait_ge(a_kz, b * 4 + (k // 4 + 1))
                        if k >= 3:
                            pe.wait_ge(a_exp, b * H1 + (k - 2))
                        for i in range(ST):
                            last = nc.tensor.matmul(SB[k % 3][:, i * S:(i + 1) * S], qT[:, i * P:(i + 1) * P],
                                                    kz[:, k, :], start=True, stop=True)
                        last.then_inc(a_s, 1)
                    h = k - 2
                    if 0 <= h < H1:
                        pe.wait_ge(a_exp, b * H1 + (h + 1))
                        if h == 1:
                            pe.wait_ge(a_ydone, b)
                        for j in range(ST):
                            for i in range(ST):
                                last = nc.tensor.transpose(TB[h % 2][:, j * S + i * P:j * S + (i + 1) * P],
                                                           prob[:, h % 3, i, j * P:(j + 1) * P], ident[:, :])
                        last.then_inc(a_t, 1)
                    h = k - 3
                    if 0 <= h:
                        if h == 0:
                            pe.wait_ge(a_v, b + 1)
                        pe.wait_ge(a_pT, b * H1 + (h + 1))
                        for i in range(ST):
                            for j in range(ST):
                                last = nc.tensor.matmul(O1[:, i, h, :], probT[:, h % 2, j, i * P:(i + 1) * P],
                                                        vaug[:, j, h, :], start=(j == 0), stop=(j == ST - 1))
                        last.then_inc(a_pv, 1)
                if not last_batch:
                    a_turn_x(b + 1)
                pe.wait_ge(a_onat, b + 1)
                for i in range(ST):
                    last = nc.tensor.transpose(TB[0][:, i * P:(i + 1) * P], onat[:, i, :], ident[:, :])
                last.then_inc(a_oT_ps, 1)
                if not last_batch:
                    a_project(b + 1)
                pe.wait_ge(a_oT, b + 1)
                for i in range(ST):
                    last = nc.tensor.matmul(TB[1][:, i * P:(i + 1) * P], oT[:, i * P:(i + 1) * P], wout_sb[:, :],
                                            start=True, stop=True)
                last.then_inc(a_y, 1)

            a_turn_x(0)
            a_project(0)
            with pe.Fori(0, NB - 1) as b:
                a_batch(b, False)
            a_batch(NB - 1, True)

            pe.wait_ge(s_wb, 16 * 6)

            def b_turn_x(b, first):
                pe.wait_ge(b_xh, b + 1)
                if not first:
                    pe.wait_ge(b_gbs, b - 1)
                for i in range(ST):
                    last = nc.tensor.transpose(Y2[:, (ST + i) * P:(ST + i + 1) * P], xh[:, i, :], ident[:, :])
                last.then_inc(b_hT_ps, 1)

            def b_project_qk(b, p):
                if p == 0:
                    pe.wait_ge(b_hT, b + 1)
                pe.wait_ge(b_q, b * NP + p)
                pe.wait_ge(b_k, b * NP + p)
                w = slice(p * P, (p + 1) * P)
                nc.tensor.matmul(QK2[:, 0:S], wq_sb[:, w], hT[:, :], start=True, stop=True)
                nc.tensor.matmul(QK2[:, S:2 * S], wk_sb[:, w], hT[:, :], start=True, stop=True).then_inc(b_qk_ps, 1)

            def b_project_v(b, p):
                for i in range(ST):
                    last = nc.tensor.matmul(VN2[:, i * P:(i + 1) * P], hT[:, i * P:(i + 1) * P],
                                            wv_sb[:, p * P:(p + 1) * P], start=True, stop=True)
                last.then_inc(b_v_ps, 1)

            def b_norms(b, p):
                pe.wait_ge(b_sq, b * NP + (p + 1))
                for i in range(ST):
                    nc.tensor.matmul(QN2[:, 2 * i:2 * i + 2], sq[:, 0, i * P:(i + 1) * P], blockones[:, 0:P:D2],
                                     start=True, stop=True)
                nc.tensor.matmul(VN2[:, S:2 * S], blockones[:, :], sq[:, 1, :], start=True, stop=True).then_inc(b_kn_ps, 1)

            def b_scores(b, p, first):
                pe.wait_ge(b_q, b * NP + (p + 1))
                pe.wait_ge(b_k, b * NP + (p + 1))
                for t in range(2):
                    h = 2 * p + t
                    if h >= 2 or not first:
                        pe.wait_ge(b_m, b * H2 + (h - 1))
                    nc.tensor.matmul(S2[t][:, 0:P], qTs[:, p % 2, 0:P], kpair[:, p % 2, t, 0:P], start=True, stop=True)
                    nc.tensor.matmul(S2[t][:, P:3 * P], qTs[:, p % 2, P:2 * P], kpair[:, p % 2, t, :],
                                     start=True, stop=True).then_inc(b_s, 1)

            def b_turn_probs(b, p, more):
                if more:
                    pe.wait_ge(b_lq, b * (2 * NP) + 2 * (p + 2))
                for t in range(2):
                    h = 2 * p + t
                    pe.wait_ge(b_exp, b * H2 + (h + 1))
                    for n in range(3):
                        last = nc.tensor.transpose(T2[t][:, n * P:(n + 1) * P], prob2[:, h % 4, n * P:(n + 1) * P],
                                                   ident[:, :])
                    last.then_inc(b_t, 1)

            def b_values(b, p):
                pe.wait_ge(b_v, b * NP + (p + 1))
                for t in range(2):
                    h = 2 * p + t
                    pe.wait_ge(b_pT, b * H2 + (h + 1))
                    if t == 0:
                        pe.wait_ge(b_oT, b * NP + p)
                    for n, (i, j) in enumerate(BLOCKS):
                        last = nc.tensor.matmul(O2[:, i, t, :], prob2T[:, t, n * P:(n + 1) * P], vpair[:, p % 4, j, t, :],
                                                start=(j == 0), stop=(j == i))
                last.then_inc(b_pv, 1)

            def b_turn_out(b, p):
                pe.wait_ge(b_onat, b * NP + (p + 1))
                for i in range(ST):
                    last = nc.tensor.transpose(OB2[:, i * P:(i + 1) * P], onat2[:, i, :], ident[:, :])
                last.then_inc(b_oT_ps, 1)

            YN = Y2[:, 2 * P:4 * P]

            def b_epilogue(b, step):
                if step == 0:
                    pe.wait_ge(b_oT, b * NP + NP)
                    pe.wait_ge(b_gbs, b)
                    for i in range(ST):
                        for p in range(NP):
                            last = nc.tensor.matmul(YN[:, i * P:(i + 1) * P], oT2[:, p, i * P:(i + 1) * P], wo_sb[:, p, :],
                                                    start=(p == 0), stop=(p == NP - 1))
                    last.then_inc(b_y, 1)
                if step == 1:
                    pe.wait_ge(b_h2n, b + 1)
                    for i in range(ST):
                        last = nc.tensor.transpose(YN[:, i * P:(i + 1) * P], h2n[:, i, :], ident[:, :])
                    last.then_inc(b_h2T_ps, 1)
                if step == 2:
                    pe.wait_ge(b_h2T, b + 1)
                    for i in range(ST):
                        last = nc.tensor.matmul(YN[:, i * NE:(i + 1) * NE], h2T[:, i * P:(i + 1) * P], gw_sb[:, :],
                                                start=True, stop=True)
                    last.then_inc(b_gl, 1)
                if step == 3:
                    pe.wait_ge(b_gate, b + 1)
                    for i in range(ST):
                        last = nc.tensor.transpose(YN[0:NE, i * P:(i + 1) * P], gnorm[:, i, :], ident[:, :])
                    last.then_inc(b_gT_ps, 1)
                if step == 4:
                    pe.wait_ge(b_gT, b + 1)
                    for i in range(ST):
                        last = nc.tensor.matmul(YN[:, i * P:(i + 1) * P], gT[:, i * P:(i + 1) * P], b2_sb[:, :],
                                                start=True, stop=True)
                    last.then_inc(b_gb, 1)

            def b_batch(b, first, last_batch):
                for p in range(NP):
                    more = p < NP - 1 or not last_batch
                    nb, np_ = (b, p + 1) if p < NP - 1 else (b + 1, 0)
                    if more:
                        b_project_qk(nb, np_)
                    b_scores(b, p, first)
                    before = p >= 1 or not first
                    pb, pp = (b, p - 1) if p >= 1 else (b - 1, NP - 1)
                    if before:
                        b_turn_probs(pb, pp, True)
                    if p >= 2:
                        b_turn_out(b, p - 2)
                    elif not first:
                        b_turn_out(b - 1, NP - 2 + p)
                    if more:
                        b_project_v(nb, np_)
                    if before:
                        pe.wait_ge(b_pT, pb * H2 + 2 * (pp + 1))
                    if more:
                        b_norms(nb, np_)
                    if before:
                        b_values(pb, pp)
                    if not first and 1 <= p <= 5:
                        b_epilogue(b - 1, p - 1)
                    if p == NP - 2 and not last_batch:
                        b_turn_x(b + 1, first)

            b_turn_x(0, True)
            b_project_qk(0, 0)
            b_project_v(0, 0)
            b_norms(0, 0)
            b_batch(0, True, False)
            with pe.Fori(1, NB - 1) as b:
                b_batch(b, False, False)
            b_batch(NB - 1, False, True)
            b_turn_probs(NB - 1, NP - 1, False)
            b_turn_out(NB - 1, NP - 2)
            b_values(NB - 1, NP - 1)
            b_turn_out(NB - 1, NP - 1)
            for step in range(5):
                b_epilogue(NB - 1, step)

            pe.wait_ge(s_wc, 32)
            pe.wait_ge(b_res, NB)
            pe.wait_ge(b_gbs, NB)
            pe.wait_ge(b_exp, NB * H2)

            def c_up(ch, e):
                for c in range(FC):
                    if e >= 1:
                        pe.wait_ge(c_hid, ch * (NE * FC) + ((e - 1) * FC + c + 1))
                    nc.tensor.matmul(HB[c][:, :], w1_sb[:, e, c * P:(c + 1) * P], hTres[:, ds(ch * CW, CW)],
                                     start=True, stop=True).then_inc(c_h, 1)

            def c_down(ch, e):
                pe.wait_ge(c_hid, ch * (NE * FC) + (e + 1) * FC)
                if e >= 2:
                    pe.wait_ge(c_acc, ch * NE + (e - 1))
                else:
                    pe.wait_ge(c_acc, ch * NE)
                for i in range(CT):
                    for c in range(FC):
                        last = nc.tensor.matmul(EB[e % 2][:, i * P:(i + 1) * P], hid[:, e % 2, c, i * P:(i + 1) * P],
                                                w2_sb[:, e * FC + c, :], start=(c == 0), stop=(c == FC - 1))
                last.then_inc(c_e, 1)

            with pe.Fori(0, NCH) as ch:
                for e in range(NE + 1):
                    if e < NE:
                        c_up(ch, e)
                    if e >= 1:
                        c_down(ch, e - 1)

        @block.scalar
        def _(act):
            def a_load_batch(b):
                act.wait_ge(a_xT_ps, b + 1)
                nc.scalar.copy(xT[:, :], VX[:, S:2 * S]).then_inc(a_xT, 1)

            def a_load_qk(b):
                act.wait_ge(a_qk_ps, b + 1)
                nc.scalar.copy(kT[:, :], QK[:, S:2 * S]).then_inc(a_kT, 1)
                nc.scalar.mul(qT[:, :], QK[:, 0:S], float(D1) ** -0.5).then_inc(a_qT, 1)

            def a_batch(b, last_batch):
                for k in range(H1):
                    act.wait_ge(a_nmax, b * H1 + (k + 1))
                    if k >= 3:
                        act.wait_ge(a_t, b * H1 + (k - 2))
                    for i in range(ST):
                        last = nc.scalar.activation(prob[:, k % 3, i, :], SB[k % 3][:, i * S:(i + 1) * S], ACT.Exp,
                                                    bias=nmax[:, k % 4, i:i + 1], scale=1.0)
                    last.then_inc(a_exp, 1)
                if not last_batch:
                    a_load_batch(b + 1)
                act.wait_ge(a_oT_ps, b + 1)
                nc.scalar.copy(oT[:, :], TB[0][:, 0:S]).then_inc(a_oT, 1)
                if not last_batch:
                    a_load_qk(b + 1)

            a_load_batch(0)
            a_load_qk(0)
            with act.Fori(0, NB - 1) as b:
                a_batch(b, False)
            a_batch(NB - 1, True)

            def b_turned_x(b):
                act.wait_ge(b_hT_ps, b + 1)
                nc.scalar.activation(hT[:, :], Y2[:, S:2 * S], ACT.Identity, bias=vcols[:, R_B:R_B + 1],
                                     scale=vcols[:, R_G:R_G + 1]).then_inc(b_hT, 1)

            def b_qk(b, p):
                act.wait_ge(b_qk_ps, b * NP + (p + 1))
                nc.scalar.activation(sq[:, :, :], QK2[:, :].rearrange("p (a s) -> p a s", a=2), ACT.Square).then_inc(b_sq, 1)
                nc.scalar.activation(qTs[:, p % 2, :], QK2[:, 0:S], ACT.Copy, scale=qks[:, p:p + 1]).then_inc(b_q, 1)

            def b_norms(b, p):
                act.wait_ge(b_kn_ps, b * NP + (p + 1))
                nc.scalar.activation(rk[:, :], VN2[:, S:2 * S], ACT.Ln, bias=eps12[:, :], scale=1.0).then_inc(b_lq, 1)
                nc.scalar.activation(lq[:, :], QN2, ACT.Ln, bias=eps12[:, :], scale=1.0).then_inc(b_lq, 1)
                act.wait_ge(b_lq, b * (2 * NP) + 2 * (p + 1))
                nc.scalar.activation(rk[:, :], rk[:, :], ACT.Exp, scale=-0.5).then_inc(b_rk, 1)
                nc.scalar.activation(rq[:, :], lq[:, :], ACT.Exp, scale=-0.5).then_inc(b_rq, 1)

            def b_exp_pair(b, p):
                for t in range(2):
                    h = 2 * p + t
                    act.wait_ge(b_m, b * H2 + (h + 1))
                    nc.scalar.activation(prob2[:, h % 4, 0:P], smask[:, h % 4, 0:P], ACT.Exp,
                                         bias=nmax2[:, h % 4, 0:1], scale=-1.0)
                    nc.scalar.activation(prob2[:, h % 4, P:3 * P], smask[:, h % 4, P:3 * P], ACT.Exp,
                                         bias=nmax2[:, h % 4, 1:2], scale=-1.0).then_inc(b_exp, 1)

            def b_out(b, p):
                act.wait_ge(b_oT_ps, b * NP + (p + 1))
                nc.scalar.copy(oT2[:, p, :], OB2[:, 0:S]).then_inc(b_oT, 1)

            def b_epilogue(b, step):
                if step == 1:
                    act.wait_ge(b_h2T_ps, b + 1)
                    act.wait_ge(b_res, b)
                    nc.scalar.activation(h2T[:, :], Y2[:, S:2 * S], ACT.Identity, bias=vcols[:, R_B:R_B + 1],
                                         scale=vcols[:, R_G:R_G + 1]).then_inc(b_h2T, 1)
                if step == 2:
                    act.wait_ge(b_glog, b + 1)
                    nc.scalar.activation(gnorm[:, :, :], glog[:, :, :], ACT.Exp).then_inc(b_gexp, 1)
                if step == 3:
                    act.wait_ge(b_gT_ps, b + 1)
                    nc.scalar.copy(gT[:, :], Y2[0:NE, S:2 * S]).then_inc(b_gT, 1)
                if step == 4:
                    act.wait_ge(b_gb, b + 1)
                    nc.scalar.copy(moe0[:, ds(b * S, S)], Y2[:, S:2 * S]).then_inc(b_gbs, 1)

            def b_batch(b, first, last_batch):
                for p in range(NP):
                    more = p < NP - 1 or not last_batch
                    nb, np_ = (b, p + 1) if p < NP - 1 else (b + 1, 0)
                    if more:
                        b_qk(nb, np_)
                    if p >= 2:
                        b_out(b, p - 2)
                    elif not first:
                        b_out(b - 1, NP - 2 + p)
                    b_exp_pair(b, p)
                    if more:
                        b_norms(nb, np_)
                    if not first and 1 <= p <= 5:
                        b_epilogue(b - 1, p - 1)
                    if p == NP - 2 and not last_batch:
                        b_turned_x(b + 1)

            act.wait_ge(s_nat, 1)
            b_turned_x(0)
            b_qk(0, 0)
            b_norms(0, 0)
            b_batch(0, True, False)
            with act.Fori(1, NB - 1) as b:
                b_batch(b, False, False)
            b_batch(NB - 1, False, True)
            b_out(NB - 1, NP - 2)
            b_out(NB - 1, NP - 1)
            for step in range(5):
                b_epilogue(NB - 1, step)

            with act.Fori(0, NCH) as ch:
                for e in range(NE):
                    for c in range(FC):
                        act.wait_ge(c_h, ch * (NE * FC) + (e * FC + c + 1))
                        if c == 0:
                            act.wait_ge(c_e, ch * NE + (e - 1)) if e >= 2 else act.wait_ge(c_e, ch * NE)
                        nc.scalar.activation(hid[:, e % 2, c, :], HB[c][:, :], ACT.Gelu_apprx_tanh,
                                             bias=vcols[:, R_B1 + e * FC + c:R_B1 + e * FC + c + 1],
                                             scale=1.0).then_inc(c_hid, 1)

        @block.vector
        def _(dve):
            link0 = Link(dve, s_link, 0)
            nc.vector.memset(vaug[:, :, :, D1:D1 + 1], 1.0)
            nc.vector.memset(vpair[:, :, :, :, D2:D2 + 1], 1.0)
            nc.vector.memset(blockones[:, :], 0.0)
            link0(nc.vector.memset(kpair[:, :, :, :], 0.0))
            nc.vector.memset(blockones[0:D2, 0:D2], 1.0).then_inc(s_const, 1)
            nc.vector.memset(blockones[D2:P, D2:P], 1.0).then_inc(s_const, 1)
            dve.wait_ge(s_vcol_ps, 1)
            link0(nc.vector.tensor_copy(vcols[:, :], bank[0][:, 0:P]))
            nc.vector.scalar_tensor_tensor(qks[:, :], vcols[:, R_QS:R_QS + NP], QK_SCALE, vcols[:, R_KS:R_KS + NP],
                                           ALU.mult, ALU.mult)
            for i, r in enumerate((R_G, R_B, R_GB)):
                last = nc.vector.tensor_copy(gspread[:, i, :], vcols[:, r:r + 1].broadcast_to([P, P]))
            last.then_inc(s_spread, 1)
            dve.wait_ge(s_nat_ps, 1)
            nc.vector.tensor_copy(gnat[:, :, :], bank[1][:, 0:2 * P].rearrange("p (a d) -> p a d", a=2))
            link0(nc.vector.tensor_copy(gbnat[:, :], bank[1][:, 2 * P:2 * P + NE]))
            nc.vector.tensor_copy(gbnat[:, 0:1], gbnat[:, 0:1]).then_inc(s_nat, 1)

            def x_tile(b, i):
                return xres[:, ds((b * ST + i) * P, P)]

            def a_norm_x(b, link):
                norm_stats(link, [x_tile(b, i) for i in range(ST)])
                for i in range(ST):
                    last = normalize(xh[:, i, :], x_tile(b, i), i)
                last.then_inc(a_xh, 1)

            def a_values(b):
                dve.wait_ge(a_v_ps, b + 1)
                nc.vector.tensor_copy(vaug[:, :, :, 0:D1], VX[:, 0:S].rearrange("p (i h d) -> p i h d", i=ST, h=H1)
                                      ).then_inc(a_v, 1)

            def a_turned(b, h):
                dve.wait_ge(a_t, b * H1 + (h + 1))
                if h >= 2:
                    dve.wait_ge(a_pv, b * H1 + (h - 1))
                nc.vector.tensor_copy(probT[:, h % 2, :, :], TB[h % 2][:, :].rearrange("p (j s) -> p j s", j=ST)
                                      ).then_inc(a_pT, 1)

            def a_batch(b, link, last_batch):
                for k in range(H1 + 2):
                    if k < H1:
                        dve.wait_ge(a_s, b * H1 + (k + 1))
                        nc.vector.tensor_reduce(nmax[:, k % 4, :], SB[k % 3][:, :].rearrange("p (i t) -> p i t", i=ST),
                                                X_AXIS, ALU.max, negate=True).then_inc(a_nmax, 1)
                    if k == 1:
                        a_values(b)
                    if k >= 2:
                        a_turned(b, k - 2)
                    if k == 8 and not last_batch:
                        a_norm_x(b + 1, link)
                dve.wait_ge(a_pv, b * H1 + H1)
                link(nc.vector.reciprocal(rsum[:, :, :], O1[:, :, :, D1]))
                nc.vector.tensor_tensor(onat[:, :, :].rearrange("p i (h d) -> p i h d", h=H1), O1[:, :, :, 0:D1],
                                        rsum[:, :, :].unsqueeze(3).broadcast_to([P, ST, H1, D1]), ALU.mult
                                        ).then_inc(a_onat, 1)
                dve.wait_ge(a_y, b + 1)
                norm_stats(link, [TB[1][:, i * P:(i + 1) * P] for i in range(ST)])
                for i in range(ST):
                    last = normalize(tmp[:, i, :], TB[1][:, i * P:(i + 1) * P], i)
                link(last)
                for i in range(ST):
                    last = nc.vector.tensor_tensor(x_tile(b, i), x_tile(b, i), tmp[:, i, :], ALU.add)
                last.then_inc(a_ydone, 1)

            for i in range(XQ):
                dve.wait_ge(s_x, 16 * XQ)
            a_norm_x(0, link0)
            A_LINKS = 2 * NORM_LINKS + 2
            with dve.Fori(0, NB - 1) as b:
                link = Link(dve, a_link, b * A_LINKS)
                a_batch(b, link, False)
                assert link.n == A_LINKS, link.n
            link = Link(dve, a_link, (NB - 1) * A_LINKS)
            a_batch(NB - 1, link, True)
            dve.wait_ge(a_ydone, NB)

            def b_norm_x(b, link):
                norm_stats(link, [x_tile(b, i) for i in range(ST)])
                for i in range(ST):
                    last = normalize(tmp[:, i, :], x_tile(b, i), i)
                link(last)
                norm_stats(link, [tmp[:, i, :] for i in range(ST)])
                for i in range(ST):
                    last = normalize(xh[:, i, :], tmp[:, i, :], i)
                last.then_inc(b_xh, 1)

            def b_keys(b, p):
                dve.wait_ge(b_lq, b * (2 * NP) + 2 * (p + 1))
                nc.vector.tensor_copy(vpair[:, p % 4, :, :, 0:D2],
                                      VN2[:, 0:S].rearrange("p (i h d) -> p i h d", i=ST, h=2)).then_inc(b_v, 1)
                dve.wait_ge(b_rk, b * NP + (p + 1))
                dve.wait_ge(b_rq, b * NP + (p + 1))
                nc.vector.tensor_scalar_mul(nrq[:, p % 2, :, :], rq[:, :].rearrange("p (i t) -> p i t", i=ST), -1.0
                                            ).then_inc(b_nrq, 1)
                for t in range(2):
                    r = slice(t * D2, (t + 1) * D2)
                    last = nc.vector.tensor_tensor(kpair[r, p % 2, t, :], QK2[r, S:2 * S], rk[r, :], ALU.mult)
                last.then_inc(b_k, 1)

            def b_maxes(b, p):
                dve.wait_ge(b_nrq, b * NP + (p + 1))
                for t in range(2):
                    h = 2 * p + t
                    dve.wait_ge(b_s, b * H2 + (h + 1))
                    carry_wait()
                    nc.vector.tensor_tensor_reduce(
                        out=smask[:, h % 4, 0:P], in0=S2[t][:, 0:P], in1=causal[:, 1, :],
                        scale=nrq[:, p % 2, 0, t:t + 1], scalar=3.0e38, op0=ALU.add, op1=ALU.min,
                        accum_out=nmax2[:, h % 4, 0:1])
                    nc.vector.tensor_tensor_reduce(
                        out=smask[:, h % 4, P:3 * P], in0=S2[t][:, P:3 * P], in1=causal[:, :, :].rearrange("p a s -> p (a s)"),
                        scale=nrq[:, p % 2, 1, t:t + 1], scalar=3.0e38, op0=ALU.add, op1=ALU.min,
                        accum_out=nmax2[:, h % 4, 1:2]).then_inc(b_m, 1)

            def b_turned(b, p):
                for t in range(2):
                    h = 2 * p + t
                    dve.wait_ge(b_t, b * H2 + (h + 1))
                    nc.vector.tensor_copy(prob2T[:, t, :], T2[t][:, 0:3 * P]).then_inc(b_pT, 1)

            def b_onat_pair(b, p, link):
                dve.wait_ge(b_pv, b * NP + (p + 1))
                link(nc.vector.reciprocal(rsum2[:, :, :], O2[:, :, :, D2]))
                dve.wait_ge(b_oT_ps, b * NP + p)
                nc.vector.tensor_tensor(onat2[:, :, :].rearrange("p i (h d) -> p i h d", h=2), O2[:, :, :, 0:D2],
                                        rsum2[:, :, :].unsqueeze(3).broadcast_to([P, ST, 2, D2]), ALU.mult
                                        ).then_inc(b_onat, 1)

            def b_epilogue(b, step, link):
                if step == 0:
                    dve.wait_ge(b_y, b + 1)
                    norm_stats(link, [Y2[:, S + i * P:S + (i + 1) * P] for i in range(ST)])
                    for i in range(ST):
                        last = normalize(h2n[:, i, :], Y2[:, S + i * P:S + (i + 1) * P], i)
                    last.then_inc(b_h2n, 1)
                if step == 2:
                    dve.wait_ge(b_gl, b + 1)
                    link(nc.vector.tensor_tensor(glog[:, :, :], Y2[:, S:S + ST * NE].rearrange("p (i e) -> p i e", i=ST),
                                                 gbnat[:, :].unsqueeze(1).broadcast_to([P, ST, NE]), ALU.add))
                    link(nc.vector.tensor_reduce(gmx[:, :], glog[:, :, :], X_AXIS, ALU.max))
                    nc.vector.tensor_tensor(glog[:, :, :], glog[:, :, :],
                                            gmx[:, :].unsqueeze(2).broadcast_to([P, ST, NE]), ALU.subtract).then_inc(b_glog, 1)
                    dve.wait_ge(b_gexp, b + 1)
                    link(nc.vector.tensor_reduce(gsm[:, :], gnorm[:, :, :], X_AXIS, ALU.add))
                    link(nc.vector.reciprocal(gmx[:, :], gsm[:, :]))
                    link(nc.vector.tensor_tensor(gnorm[:, :, :], gnorm[:, :, :],
                                                 gmx[:, :].unsqueeze(2).broadcast_to([P, ST, NE]), ALU.mult))
                    nc.vector.tensor_copy(gates[:, ds(b * (ST * NE), ST * NE)],
                                          gnorm[:, :, :].rearrange("p i e -> p (i e)")).then_inc(b_gate, 1)

            def b_batch(b, link, first, last_batch):
                for p in range(NP):
                    more = p < NP - 1 or not last_batch
                    nb, np_ = (b, p + 1) if p < NP - 1 else (b + 1, 0)
                    b_maxes(b, p)
                    if p >= 1:
                        b_turned(b, p - 1)
                    elif not first:
                        b_turned(b - 1, NP - 1)
                    if more:
                        b_keys(nb, np_)
                    if p >= 1:
                        b_onat_pair(b, p - 1, link)
                    elif not first:
                        b_onat_pair(b - 1, NP - 1, link)
                    if not first and 1 <= p <= 5:
                        b_epilogue(b - 1, p - 1, link)
                    if p == 4 and not last_batch:
                        b_norm_x(b + 1, link)

            b_norm_x(0, link0)
            b_keys(0, 0)
            n_first = (NP - 1) + (2 * NORM_LINKS + 1)
            B_LINKS = n_first + 1 + (NORM_LINKS + 5)
            link = Link(dve, b_link, 0)
            b_batch(0, link, True, False)
            assert link.n == n_first, link.n
            with dve.Fori(1, NB - 1) as b:
                link = Link(dve, b_link, (b - 1) * B_LINKS + n_first)
                b_batch(b, link, False, False)
                assert link.n == B_LINKS, (link.n, B_LINKS)
            link = Link(dve, b_link, (NB - 2) * B_LINKS + n_first)
            b_batch(NB - 1, link, False, True)
            b_turned(NB - 1, NP - 1)
            b_onat_pair(NB - 1, NP - 1, link)
            for step in range(5):
                b_epilogue(NB - 1, step, link)

            dve.wait_ge(b_gbs, NB)
            dve.wait_ge(b_gate, NB)

            def c_chunk(ch, half, link):
                dve.wait_ge(c_fin, ch)
                nc.vector.tensor_copy(gch[:, :, :], gates[:, ds(ch * (CT * NE), CT * NE)].rearrange("p (i e) -> p i e", i=CT))
                link(nc.vector.tensor_copy(acc[:, :, :], moe0[:, ds(ch * CW, CW)].rearrange("p (i d) -> p i d", i=CT)))
                for e in range(NE):
                    dve.wait_ge(c_e, ch * NE + (e + 1))
                    for i in range(CT):
                        last = nc.vector.scalar_tensor_tensor(acc[:, i, :], EB[e % 2][:, i * P:(i + 1) * P],
                                                              gch[:, i, e:e + 1], acc[:, i, :], ALU.mult, ALU.add)
                    last.then_inc(c_acc, 1)
                    dve.wait_ge(c_acc, ch * NE + (e + 1))
                norm_stats(link, [acc[:, i, :] for i in range(CT)])
                for i in range(CT):
                    last = normalize(tmp[:, i, :], acc[:, i, :], i)
                link(last)
                link(nc.vector.tensor_tensor(acc[:, :, :], tmp[:, :, :],
                                             gnat[:, 0:1, :].broadcast_to([P, CT, P]), ALU.mult))
                link(nc.vector.tensor_tensor(tmp[:, :, :], acc[:, :, :],
                                             gnat[:, 1:2, :].broadcast_to([P, CT, P]), ALU.add))
                norm_stats(link, [tmp[:, i, :] for i in range(CT)])
                for i in range(CT):
                    last = normalize(acc[:, i, :], tmp[:, i, :], i)
                link(last)
                return nc.vector.tensor_tensor(fin[:, half, :, :], acc[:, :, :],
                                               xres[:, ds(ch * CW, CW)].rearrange("p (i d) -> p i d", i=CT), ALU.add)

            C_LINKS = 2 * NORM_LINKS + 5
            with dve.Fori(0, NCH // 2) as ii:
                link = Link(dve, c_link, ii * (2 * C_LINKS))
                for j in range(2):
                    if j == 0:
                        dve.wait_ge(s_out, ii * 32)
                    c_chunk(ii * 2 + j, j, link).then_inc(c_fin, 1)
                assert link.n == 2 * C_LINKS, link.n


_INS = ['L0_attn_x', 'L0_attn_w_qkv', 'L0_attn_w_out', 'L0_ffn_ln_g', 'L0_ffn_ln_b', 'L0_ffn_Wq', 'L0_ffn_Wk', 'L0_ffn_Wv',
        'L0_ffn_q_scale', 'L0_ffn_k_scale', 'L0_ffn_Wo', 'L0_ffn_gate_w', 'L0_ffn_gate_b', 'L0_ffn_w1', 'L0_ffn_b1',
        'L0_ffn_w2', 'L0_ffn_b2']


def kernel(**inputs):
    import numpy as _np
    import concourse.bacc as _bacc
    from concourse import mybir as _mybir
    from concourse.bass_utils import run_bass_kernel_spmd as _run

    nc = _bacc.Bacc("TRN2", target_bir_lowering=False, num_devices=1)
    arrays, args = {}, []
    for name in _INS:
        a = _np.ascontiguousarray(inputs[name])
        arrays[f"in_{name}"] = a
        args.append(nc.dram_tensor(f"in_{name}", a.shape, _mybir.dt.from_np(a.dtype), kind="ExternalInput").ap())
    shape = inputs['L0_attn_x'].shape
    args.append(nc.dram_tensor("out_0", shape, _mybir.dt.float32, kind="ExternalOutput").ap())
    sandwich_kernel(nc, *args)
    r = _run(nc, [arrays], core_ids=[0])
    return r.results[0]["out_0"]
```

```python
from contextlib import ExitStack

import concourse.bass as bass
from concourse import mybir

F32 = mybir.dt.float32
I32 = mybir.dt.int32
ALU = mybir.AluOpType
ACT = mybir.ActivationFunctionType
X_AXIS = mybir.AxisListType.X

P = 128
LN_EPS = 1e-5
L2_EPS = 1e-12
QK_SCALE = 10.0
MASKED = -1.0e30
RSQRT_MAGIC = float(0x5F3759DF)
NORM_LINKS = 14


def ds(start, size):
    return bass.ds(start, size)


class Link:

    def __init__(self, engine, sem, base):
        self.engine, self.sem, self.base, self.n = engine, sem, base, 0

    def __call__(self, instruction):
        self.n += 1
        instruction.then_inc(self.sem, 1)
        self.engine.wait_ge(self.sem, self.base + self.n)


def sandwich_kernel(nc, x, w_qkv, w_out, ln_g, ln_b, Wq, Wk, Wv, q_scale, k_scale, Wo, gate_w, gate_b,
                    w1, b1, w2, b2, out):
    NB, S, E = x.shape
    ST = S // P
    NT = NB * ST
    H1 = 16
    D1 = E // H1
    H2, _, D2 = q_scale.shape
    NP = H2 * D2 // P
    NE, _, FF = w1.shape
    FC = FF // P
    assert E == P and ST == 2 and D2 * 2 == P and H2 == 2 * NP
    CT = 4
    NCH = NT // CT
    CW = CT * P

    ctx = ExitStack()
    with ctx:
        def sb(name, shape, dt=F32):
            return ctx.enter_context(nc.sbuf_tensor(name, shape, dt))

        def sem(name):
            return ctx.enter_context(nc.semaphore(name))

        bank = [ctx.enter_context(nc.psum_tensor(f"bank{i}", [P, 512], F32)) for i in range(8)]

        xres = sb("xres", [P, NT * P])
        hTres = sb("hTres", [P, NT * P])
        moe0 = sb("moe0", [P, NT * P])
        gates = sb("gates", [P, NT * NE])
        wqkv_sb = sb("wqkv_sb", [P, 3 * E])
        wout_sb = sb("wout_sb", [P, E])
        wq_sb = sb("wq_sb", [P, H2 * D2])
        wk_sb = sb("wk_sb", [P, H2 * D2])
        wv_sb = sb("wv_sb", [P, H2 * D2])
        wo_sb = sb("wo_sb", [P, NP, E])
        gw_sb = sb("gw_sb", [P, NE])
        w1_sb = sb("w1_sb", [P, NE, FF])
        w2_sb = sb("w2_sb", [P, NE * FC, E])
        b2_sb = sb("b2_sb", [NE, E])
        R_B1, R_QS, R_KS, R_G, R_B, R_GB = 0, NE * FC, NE * FC + NP, NE * FC + 2 * NP, NE * FC + 2 * NP + 1, NE * FC + 2 * NP + 2
        vrows = sb("vrows", [P, P])
        vcols = sb("vcols", [P, P])
        qks = sb("qks", [P, NP])
        gspread = sb("gspread", [P, 3, P])
        gnat = sb("gnat", [P, 2, P])
        gbnat = sb("gbnat", [P, NE])
        ident = sb("ident", [P, P])
        headmask = sb("headmask", [P, H1])
        causal = sb("causal", [P, 2, P])
        blockones = sb("blockones", [P, P])
        eps12 = sb("eps12", [P, 1])

        bst = sb("bst", [P, CT, 6])
        mv = sb("mv", [P, CT, 2])
        pad = sb("pad", [P, 64])
        bst3 = sb("bst3", [P, 3, ST, 6])
        mv3 = sb("mv3", [P, 3, ST, 2])
        rstd3 = sb("rstd3", [P, 3, ST])
        epsln = sb("epsln", [P, 1])
        rs_v = sb("rs_v", [P, CT])
        rs_t = sb("rs_t", [P, CT], I32)
        rs_i = sb("rs_i", [P, CT], I32)
        rs_a = sb("rs_a", [P, CT])
        rs_y = sb("rs_y", [P, CT])

        xh = sb("xh", [P, ST, P])
        xT = sb("xT", [P, S])
        qT = sb("qT", [P, S])
        kT = sb("kT", [P, S])
        kz = sb("kz", [P, H1, S])
        vaug = sb("vaug", [P, ST, H1, D1 + 1])
        nmax = sb("nmax", [P, 4, ST])
        prob = sb("prob", [P, 3, ST, S])
        probT = sb("probT", [P, 2, ST, S])
        rsum = sb("rsum", [P, ST, H1])
        onat = sb("onat", [P, ST, P])
        oT = sb("oT", [P, S])
        tmp = sb("tmp", [P, CT, P])

        hT = sb("hT", [P, S])
        qTs = sb("qTs", [P, 2, S])
        sq = sb("sq", [P, 2, S])
        rr = sb("rr", [P, 2, S])
        kpair = sb("kpair", [P, 2, 2, S])
        vpair = sb("vpair", [P, 4, ST, P])
        smask = sb("smask", [P, 4, 3 * P])
        nmax2 = sb("nmax2", [P, 4, ST])
        prob2 = sb("prob2", [P, 4, 3 * P])
        prob2T = sb("prob2T", [P, 2, 2, 3 * P])
        sums = sb("sums", [P, 2, 2, ST])
        rblk = sb("rblk", [P, 2, 2, 3])
        oT2 = sb("oT2", [P, NP, S])
        h2n = sb("h2n", [P, ST, P])
        h2T = sb("h2T", [P, S])
        glog = sb("glog", [P, ST, NE])
        gmx = sb("gmx", [P, ST])
        gsm = sb("gsm", [P, ST])
        gnorm = sb("gnorm", [P, ST, NE])
        gT = sb("gT", [NE, S])

        hid = sb("hid", [P, 2, FC, CW])
        acc = sb("acc", [P, CT, P])
        gch = sb("gch", [P, CT, NE])
        fin = sb("fin", [P, 2, CT, P])

        s_x, s_wa, s_wb, s_wc, s_vec, s_out = (sem(n) for n in ("s_x", "s_wa", "s_wb", "s_wc", "s_vec", "s_out"))
        s_vz, s_const, s_zero, s_vcol_ps, s_vcols, s_spread, s_nat_ps, s_nat = (
            sem(n) for n in ("s_vz", "s_const", "s_zero", "s_vcol_ps", "s_vcols", "s_spread", "s_nat_ps", "s_nat"))
        s_cst1 = sem("s_cst1")
        s_link = sem("s_link")
        a_xh, a_xT_ps, a_xT, a_qk_ps, a_v_ps, a_qT, a_kT, a_kz, a_v = (
            sem("a_" + n) for n in ("xh", "xT_ps", "xT", "qk_ps", "v_ps", "qT", "kT", "kz", "v"))
        a_s, a_nmax, a_exp, a_t, a_pT, a_pv, a_onat, a_oT_ps, a_oT, a_y, a_ydone, a_link = (
            sem("a_" + n) for n in ("s", "nmax", "exp", "t", "pT", "pv", "onat", "oT_ps", "oT", "y", "ydone", "link"))
        b_xh, b_hT_ps, b_hT, b_qk_ps, b_sq, b_n_ps, b_ln, b_rr, b_k, b_v_ps, b_v = (
            sem("b_" + n) for n in ("xh", "hT_ps", "hT", "qk_ps", "sq", "n_ps", "ln", "rr", "k", "v_ps", "v"))
        b_s, b_m, b_exp, b_rec, b_pn, b_t, b_pT, b_pv, b_oT, b_y, b_link = (
            sem("b_" + n) for n in ("s", "m", "exp", "rec", "pn", "t", "pT", "pv", "oT", "y", "link"))
        b_mv, b_lnv, b_rstd = ([sem(f"b_{n}{i}") for i in range(3)] for n in ("mv", "lnv", "rstd"))
        b_h2n, b_h2T_ps, b_h2T, b_gl, b_glog, b_gexp, b_gate, b_gT_ps, b_gT, b_gb, b_gbs, b_res = (
            sem("b_" + n) for n in ("h2n", "h2T_ps", "h2T", "gl", "glog", "gexp", "gate", "gT_ps", "gT", "gb", "gbs", "res"))
        c_h, c_hid, c_e, c_acc, c_link, c_fin = (sem("c_" + n) for n in ("h", "hid", "e", "acc", "link", "fin"))

        block = ctx.enter_context(nc.Block())

        XQ = 4
        x_rows = x.rearrange("b (i p) e -> p (b i) e", p=P)
        out_rows = out.rearrange("b (i p) e -> p (b i) e", p=P)
        xres_t = xres[:, :].rearrange("p (t e) -> p t e", e=P)

        @block.sync
        def _(sp):
            sp.wait_ge(s_vz, 1)
            n = NT // XQ
            sp.dma_start(xres_t[:, 0:n, :], x_rows[:, 0:n, :]).then_inc(s_x, 16)
            sp.dma_start(wqkv_sb[:, :], w_qkv).then_inc(s_wa, 16)
            sp.dma_start(wout_sb[:, :], w_out).then_inc(s_wa, 16)
            for i in range(1, XQ):
                sp.dma_start(xres_t[:, i * n:(i + 1) * n, :], x_rows[:, i * n:(i + 1) * n, :]).then_inc(s_x, 16)
            sp.dma_start(vrows[R_B1:R_B1 + NE * FC, :], b1.rearrange("e (c f) -> (e c) f", f=P)).then_inc(s_vec, 16)
            sp.dma_start(vrows[R_QS:R_QS + NP, :], q_scale.rearrange("(p t) o d -> p (t o d)", t=2)).then_inc(s_vec, 16)
            sp.dma_start(vrows[R_KS:R_KS + NP, :], k_scale.rearrange("(p t) o d -> p (t o d)", t=2)).then_inc(s_vec, 16)
            sp.dma_start(vrows[R_G:R_G + 1, :], ln_g.rearrange("(a d) -> a d", a=1)).then_inc(s_vec, 16)
            sp.dma_start(vrows[R_B:R_B + 1, :], ln_b.rearrange("(a d) -> a d", a=1)).then_inc(s_vec, 16)
            sp.dma_start(vrows[R_GB:R_GB + 1, 0:NE], gate_b.rearrange("(a d) -> a d", a=1)).then_inc(s_vec, 16)
            for w_sb, w in ((wq_sb, Wq), (wk_sb, Wk), (wv_sb, Wv), (gw_sb, gate_w), (b2_sb, b2)):
                sp.dma_start(w_sb[:, :], w).then_inc(s_wb, 16)
            sp.dma_start(wo_sb[:, :, :], Wo.rearrange("(k p) e -> p k e", p=P)).then_inc(s_wb, 16)
            sp.dma_start(w1_sb[:, :, :], w1.rearrange("e d f -> d e f")).then_inc(s_wc, 16)
            sp.dma_start(w2_sb[:, :, :], w2.rearrange("e (c f) d -> f (e c) d", f=P)).then_inc(s_wc, 16)
            sp.sem_inc(s_out, 16)
            with sp.Fori(0, NCH // 2) as ii:
                for j in range(2):
                    sp.wait_ge(c_fin, ii * 2 + (j + 2))
                    sp.dma_start(out_rows[:, ds(ii * (2 * CT) + j * CT, CT), :], fin[:, j, :, :]).then_inc(s_out, 16)
            sp.wait_ge(s_out, 16 * (NCH + 1))

        @block.gpsimd
        def _(pool):
            pool.sem_inc(b_res, 1)
            nc.gpsimd.memset(vrows[:, :], 0.0).then_inc(s_vz, 1)
            nc.gpsimd.memset(ident[:, :], 0.0).then_inc(s_cst1, 1)
            nc.gpsimd.memset(headmask[:, :], 1.0).then_inc(s_cst1, 1)
            nc.gpsimd.memset(causal[:, :, :], 0.0).then_inc(s_cst1, 1)
            nc.gpsimd.memset(eps12[:, :], L2_EPS).then_inc(s_const, 1)
            nc.gpsimd.memset(epsln[:, :], LN_EPS).then_inc(s_const, 1)
            pool.wait_ge(s_cst1, 3)
            nc.gpsimd.affine_select(out=ident[:, :], in_=ident[:, :], compare_op=ALU.not_equal, fill=1.0,
                                    base=0, pattern=[[-1, P]], channel_multiplier=1).then_inc(s_const, 1)
            nc.gpsimd.affine_select(out=headmask[:, :], in_=headmask[:, :], compare_op=ALU.is_ge, fill=0.0,
                                    base=0, pattern=[[-D1, H1]], channel_multiplier=1).then_inc(s_cst1, 1)
            pool.wait_ge(s_cst1, 4)
            nc.gpsimd.affine_select(out=headmask[:, :], in_=headmask[:, :], compare_op=ALU.is_ge, fill=0.0,
                                    base=D1 - 1, pattern=[[D1, H1]], channel_multiplier=-1).then_inc(s_const, 1)
            nc.gpsimd.affine_select(out=causal[:, 1, :], in_=causal[:, 1, :], compare_op=ALU.is_ge, fill=MASKED,
                                    base=0, pattern=[[-1, P]], channel_multiplier=1).then_inc(s_const, 1)

            pool.wait_ge(s_const, 7)
            HG = 4

            def mask_keys(b):
                pool.wait_ge(a_kT, b + 1)
                for j in range(H1 // HG):
                    nc.gpsimd.tensor_tensor(
                        kz[:, HG * j:HG * (j + 1), :],
                        kT[:, :].unsqueeze(1).broadcast_to([P, HG, S]),
                        headmask[:, HG * j:HG * (j + 1)].unsqueeze(2).broadcast_to([P, HG, S]),
                        ALU.mult).then_inc(a_kz, 1)

            with pool.Fori(0, NB) as b:
                mask_keys(b)
            def b_normalize(b, p):
                pool.wait_ge(b_rec, b * NP + (p + 1))
                for t in range(2):
                    pr = prob2[:, (2 * p + t) % 4, :].rearrange("q (n s) -> q n s", n=3)
                    nc.gpsimd.tensor_tensor(pr, pr, rblk[:, p % 2, t, :].unsqueeze(2).broadcast_to([P, 3, P]),
                                            ALU.mult).then_inc(b_pn, 1)

            def b_keep_input(b):
                pool.wait_ge(b_h2T, b + 1)
                nc.gpsimd.tensor_copy(hTres[:, ds(b * S, S)], h2T[:, :]).then_inc(b_res, 1)

            for p in range(NP):
                b_normalize(0, p)
            with pool.Fori(1, NB) as b:
                for p in range(NP):
                    b_normalize(b, p)
                    if p == 3:
                        b_keep_input(b - 1)
            b_keep_input(NB - 1)

        carried = [0]

        def carry_wait():
            carried[0] += 1
            nc.vector.memset(pad[:, carried[0] % 64:carried[0] % 64 + 1], 0.0)

        def rsqrt_steps(link, n, var, eps):
            v, t, i, a, y = (q[:, 0:n] for q in (rs_v, rs_t, rs_i, rs_a, rs_y))
            link(nc.vector.tensor_scalar_add(v, var, eps))
            link(nc.vector.tensor_single_scalar(t, v.bitcast(I32), 1, ALU.arith_shift_right))
            link(nc.vector.tensor_scalar(i, t, -1.0, RSQRT_MAGIC, ALU.mult, ALU.add))
            guess = i.bitcast(F32)
            for step in range(3):
                yy = guess if step == 0 else y
                link(nc.vector.tensor_tensor(a, yy, yy, ALU.mult))
                link(nc.vector.scalar_tensor_tensor(a, a, -0.5, v, ALU.mult, ALU.mult))
                link(nc.vector.scalar_tensor_tensor(y, a, 1.5, yy, ALU.add, ALU.mult))

        def norm_stats(link, tiles):
            n = len(tiles)
            for i, tile in enumerate(tiles):
                last = nc.vector.bn_stats(bst[:, i, :], tile)
            link(last)
            carry_wait()
            for i in range(n):
                last = nc.vector.bn_aggr(mv[:, i, :], bst[:, i, :])
            link(last)
            rsqrt_steps(link, n, mv[:, 0:n, 1], LN_EPS)

        def normalize(dst, src, i):
            return nc.vector.tensor_scalar(dst, src, mv[:, i, 0:1], rs_y[:, i:i + 1], ALU.subtract, ALU.mult)

        SB, TB = bank[0:3], bank[3:5]
        QK, VX, OB = bank[5], bank[6], bank[7]
        O1 = OB[:, 0:ST * H1 * (D1 + 1)].rearrange("p (i h d) -> p i h d", i=ST, h=H1)
        S2, T2 = bank[0:2], bank[3:5]
        QK2, N2, OV2, Y2 = bank[5], bank[6], bank[7], bank[2]
        HB, EB = bank[0:4], bank[4:6]

        BLOCKS = ((0, 0), (1, 0), (1, 1))

        @block.tensor
        def _(pe):
            pe.sem_inc(c_e, 1)
            pe.wait_ge(s_const, 7)
            pe.wait_ge(s_vec, 16 * 6)
            nc.tensor.transpose(bank[0][:, 0:P], vrows[:, :], ident[:, :]).then_inc(s_vcol_ps, 1)
            pe.wait_ge(s_spread, 1)
            for i in range(3):
                last = nc.tensor.transpose(bank[1][:, i * P:(i + 1) * P], gspread[:, i, :], ident[:, :])
            last.then_inc(s_nat_ps, 1)
            pe.wait_ge(s_nat, 1)
            pe.wait_ge(s_wa, 32)

            def a_turn_x(b):
                pe.wait_ge(a_xh, b + 1)
                for i in range(ST):
                    last = nc.tensor.transpose(VX[:, (ST + i) * P:(ST + i + 1) * P], xh[:, i, :], ident[:, :])
                last.then_inc(a_xT_ps, 1)

            def a_project(b):
                pe.wait_ge(a_xT, b + 1)
                nc.tensor.matmul(QK[:, 0:S], wqkv_sb[:, 0:E], xT[:, :], start=True, stop=True)
                nc.tensor.matmul(QK[:, S:2 * S], wqkv_sb[:, E:2 * E], xT[:, :], start=True, stop=True).then_inc(a_qk_ps, 1)
                for i in range(ST):
                    last = nc.tensor.matmul(VX[:, i * P:(i + 1) * P], xT[:, i * P:(i + 1) * P],
                                            wqkv_sb[:, 2 * E:3 * E], start=True, stop=True)
                last.then_inc(a_v_ps, 1)

            def a_batch(b, last_batch):
                pe.wait_ge(a_qT, b + 1)
                for k in range(H1 + 3):
                    if k < H1:
                        if k % 4 == 0:
                            pe.wait_ge(a_kz, b * 4 + (k // 4 + 1))
                        if k >= 3:
                            pe.wait_ge(a_exp, b * H1 + (k - 2))
                        for i in range(ST):
                            last = nc.tensor.matmul(SB[k % 3][:, i * S:(i + 1) * S], qT[:, i * P:(i + 1) * P],
                                                    kz[:, k, :], start=True, stop=True)
                        last.then_inc(a_s, 1)
                    h = k - 2
                    if 0 <= h < H1:
                        pe.wait_ge(a_exp, b * H1 + (h + 1))
                        if h == 1:
                            pe.wait_ge(a_ydone, b + 1)
                        for j in range(ST):
                            for i in range(ST):
                                last = nc.tensor.transpose(TB[h % 2][:, j * S + i * P:j * S + (i + 1) * P],
                                                           prob[:, h % 3, i, j * P:(j + 1) * P], ident[:, :])
                        last.then_inc(a_t, 1)
                    h = k - 3
                    if 0 <= h:
                        if h == 0:
                            pe.wait_ge(a_v, b + 1)
                        pe.wait_ge(a_pT, b * H1 + (h + 1))
                        for i in range(ST):
                            for j in range(ST):
                                last = nc.tensor.matmul(O1[:, i, h, :], probT[:, h % 2, j, i * P:(i + 1) * P],
                                                        vaug[:, j, h, :], start=(j == 0), stop=(j == ST - 1))
                        last.then_inc(a_pv, 1)
                if not last_batch:
                    a_turn_x(b + 1)
                pe.wait_ge(a_onat, b + 1)
                for i in range(ST):
                    last = nc.tensor.transpose(TB[0][:, i * P:(i + 1) * P], onat[:, i, :], ident[:, :])
                last.then_inc(a_oT_ps, 1)
                if not last_batch:
                    a_project(b + 1)
                pe.wait_ge(a_oT, b + 1)
                for i in range(ST):
                    last = nc.tensor.matmul(TB[1][:, i * P:(i + 1) * P], oT[:, i * P:(i + 1) * P], wout_sb[:, :],
                                            start=True, stop=True)
                last.then_inc(a_y, 1)

            a_turn_x(0)
            a_project(0)
            with pe.Fori(0, NB - 1) as b:
                a_batch(b, False)
            a_batch(NB - 1, True)

            pe.wait_ge(s_wb, 16 * 6)

            def b_turn_x(b, start):
                pe.wait_ge(b_xh, b + 1)
                if not start:
                    pe.wait_ge(b_ln, b * NP)
                for i in range(ST):
                    last = nc.tensor.transpose(N2[:, i * P:(i + 1) * P], xh[:, i, :], ident[:, :])
                last.then_inc(b_hT_ps, 1)

            def b_project_qk(b, p):
                if p == 0:
                    pe.wait_ge(b_hT, b + 1)
                pe.wait_ge(b_k, b * NP + p)
                w = slice(p * P, (p + 1) * P)
                nc.tensor.matmul(QK2[:, 0:S], wq_sb[:, w], hT[:, :], start=True, stop=True)
                nc.tensor.matmul(QK2[:, S:2 * S], wk_sb[:, w], hT[:, :], start=True, stop=True).then_inc(b_qk_ps, 1)

            def b_project_v(b, p, early):
                if not early:
                    pe.wait_ge(b_oT, b * NP + (p - 3))
                for i in range(ST):
                    last = nc.tensor.matmul(OV2[:, S + i * P:S + (i + 1) * P], hT[:, i * P:(i + 1) * P],
                                            wv_sb[:, p * P:(p + 1) * P], start=True, stop=True)
                last.then_inc(b_v_ps, 1)

            def b_norms(b, p):
                pe.wait_ge(b_sq, b * NP + (p + 1))
                nc.tensor.matmul(N2[:, :], blockones[:, :], sq[:, :, :].rearrange("p a s -> p (a s)"),
                                 start=True, stop=True).then_inc(b_n_ps, 1)

            def b_scores(b, p, t, first):
                h = 2 * p + t
                if h >= 2 or not first:
                    pe.wait_ge(b_m, b * H2 + (h - 1))
                nc.tensor.matmul(S2[t][:, 0:P], qTs[:, p % 2, 0:P], kpair[:, p % 2, t, 0:P], start=True, stop=True)
                nc.tensor.matmul(S2[t][:, P:3 * P], qTs[:, p % 2, P:2 * P], kpair[:, p % 2, t, :],
                                 start=True, stop=True).then_inc(b_s, 1)

            def b_turn_probs(b, p, first):
                for t in range(2):
                    h = 2 * p + t
                    pe.wait_ge(b_pn, b * H2 + (h + 1))
                    if t == 0 and not first:
                        pe.wait_ge(b_pT, b * H2 + h)
                    for n in range(3):
                        last = nc.tensor.transpose(T2[t][:, n * P:(n + 1) * P], prob2[:, h % 4, n * P:(n + 1) * P],
                                                   ident[:, :])
                    last.then_inc(b_t, 1)

            def b_values(b, p, first):
                if not first:
                    pe.wait_ge(b_oT, b * NP + p)
                pe.wait_ge(b_pT, b * H2 + 2 * (p + 1))
                for j in range(ST):
                    for t in range(2):
                        last = nc.tensor.matmul(OV2[t * D2:(t + 1) * D2, j * P:S], vpair[:, p % 4, j, t * D2:(t + 1) * D2],
                                                prob2T[:, p % 2, t, 2 * j * P:(2 + j) * P], start=(j == 0), stop=(j == 1))
                last.then_inc(b_pv, 1)

            YN = Y2[:, 0:S]

            def b_epilogue(b, step):
                if step == 2:
                    pe.wait_ge(b_oT, b * NP + NP)
                    pe.wait_ge(b_gbs, b + 1)
                    for i in range(ST):
                        for p in range(NP):
                            last = nc.tensor.matmul(YN[:, i * P:(i + 1) * P], oT2[:, p, i * P:(i + 1) * P], wo_sb[:, p, :],
                                                    start=(p == 0), stop=(p == NP - 1))
                    last.then_inc(b_y, 1)
                if step == 3:
                    pe.wait_ge(b_h2n, b + 1)
                    for i in range(ST):
                        last = nc.tensor.transpose(YN[:, i * P:(i + 1) * P], h2n[:, i, :], ident[:, :])
                    last.then_inc(b_h2T_ps, 1)
                if step == 4:
                    pe.wait_ge(b_h2T, b + 1)
                    for i in range(ST):
                        last = nc.tensor.matmul(YN[:, i * NE:(i + 1) * NE], h2T[:, i * P:(i + 1) * P], gw_sb[:, :],
                                                start=True, stop=True)
                    last.then_inc(b_gl, 1)
                if step == 5:
                    pe.wait_ge(b_gate, b + 1)
                    for i in range(ST):
                        last = nc.tensor.transpose(YN[0:NE, i * P:(i + 1) * P], gnorm[:, i, :], ident[:, :])
                    last.then_inc(b_gT_ps, 1)
                if step == 6:
                    pe.wait_ge(b_gT, b + 1)
                    for i in range(ST):
                        last = nc.tensor.matmul(YN[:, i * P:(i + 1) * P], gT[:, i * P:(i + 1) * P], b2_sb[:, :],
                                                start=True, stop=True)
                    last.then_inc(b_gb, 1)

            def back(b, p, n):
                return (b, p - n) if p >= n else (b - 1, p - n + NP)

            def b_batch(b, first, last_batch):
                for p in range(NP):
                    more = p < NP - 1 or not last_batch
                    nb, np_ = (b, p + 1) if p < NP - 1 else (b + 1, 0)
                    if more:
                        b_project_qk(nb, np_)
                    else:
                        pe.wait_ge(b_k, b * NP + (p + 1))
                    b_scores(b, p, 0, first)
                    if more:
                        b_project_v(nb, np_, first and p < 3)
                        b_norms(nb, np_)
                    b_scores(b, p, 1, first)
                    if not first or p >= 1:
                        b_turn_probs(*back(b, p, 1), first and p == 1)
                    if not first or p >= 2:
                        if more:
                            pe.wait_ge(b_v, nb * NP + (np_ + 1))
                        b_values(*back(b, p, 2), first and p == 2)
                    if not first:
                        b_epilogue(b - 1, p)
                    if p == NP - 2 and not last_batch:
                        b_turn_x(b + 1, False)

            b_turn_x(0, True)
            b_project_qk0 = slice(0, P)
            pe.wait_ge(b_hT, 1)
            nc.tensor.matmul(QK2[:, 0:S], wq_sb[:, b_project_qk0], hT[:, :], start=True, stop=True)
            nc.tensor.matmul(QK2[:, S:2 * S], wk_sb[:, b_project_qk0], hT[:, :], start=True, stop=True).then_inc(b_qk_ps, 1)
            b_project_v(0, 0, True)
            b_norms(0, 0)
            b_batch(0, True, False)
            with pe.Fori(1, NB - 1) as b:
                b_batch(b, False, False)
            b_batch(NB - 1, False, True)
            b_turn_probs(NB - 1, NP - 1, False)
            b_values(NB - 1, NP - 2, False)
            b_values(NB - 1, NP - 1, False)
            for step in range(NP):
                b_epilogue(NB - 1, step)

            pe.wait_ge(s_wc, 32)
            pe.wait_ge(b_res, NB + 1)
            pe.wait_ge(b_gbs, NB + 1)
            pe.wait_ge(b_exp, NB * H2)

            def c_up(ch, e):
                for c in range(FC):
                    if e >= 1:
                        pe.wait_ge(c_hid, ch * (NE * FC) + ((e - 1) * FC + c + 1))
                    nc.tensor.matmul(HB[c][:, :], w1_sb[:, e, c * P:(c + 1) * P], hTres[:, ds(ch * CW, CW)],
                                     start=True, stop=True).then_inc(c_h, 1)

            def c_down(ch, e):
                pe.wait_ge(c_hid, ch * (NE * FC) + (e + 1) * FC)
                if e >= 2:
                    pe.wait_ge(c_acc, ch * NE + e)
                else:
                    pe.wait_ge(c_acc, ch * NE + 1)
                for i in range(CT):
                    for c in range(FC):
                        last = nc.tensor.matmul(EB[e % 2][:, i * P:(i + 1) * P], hid[:, e % 2, c, i * P:(i + 1) * P],
                                                w2_sb[:, e * FC + c, :], start=(c == 0), stop=(c == FC - 1))
                last.then_inc(c_e, 1)

            with pe.Fori(0, NCH) as ch:
                for e in range(NE + 1):
                    if e < NE:
                        c_up(ch, e)
                    if e >= 1:
                        c_down(ch, e - 1)

        @block.scalar
        def _(act):
            act.sem_inc(b_gbs, 1)
            nc.scalar.preload_act_table_set("natural_log_exp_and_others")
            def a_load_batch(b):
                act.wait_ge(a_xT_ps, b + 1)
                nc.scalar.copy(xT[:, :], VX[:, S:2 * S]).then_inc(a_xT, 1)

            def a_load_qk(b):
                act.wait_ge(a_qk_ps, b + 1)
                nc.scalar.copy(kT[:, :], QK[:, S:2 * S]).then_inc(a_kT, 1)
                nc.scalar.mul(qT[:, :], QK[:, 0:S], float(D1) ** -0.5).then_inc(a_qT, 1)

            def a_batch(b, last_batch):
                for k in range(H1):
                    act.wait_ge(a_nmax, b * H1 + (k + 1))
                    if k >= 3:
                        act.wait_ge(a_t, b * H1 + (k - 2))
                    for i in range(ST):
                        last = nc.scalar.activation(prob[:, k % 3, i, :], SB[k % 3][:, i * S:(i + 1) * S], ACT.Exp,
                                                    bias=nmax[:, k % 4, i:i + 1], scale=1.0)
                    last.then_inc(a_exp, 1)
                if not last_batch:
                    a_load_batch(b + 1)
                act.wait_ge(a_oT_ps, b + 1)
                nc.scalar.copy(oT[:, :], TB[0][:, 0:S]).then_inc(a_oT, 1)
                if not last_batch:
                    a_load_qk(b + 1)

            a_load_batch(0)
            a_load_qk(0)
            with act.Fori(0, NB - 1) as b:
                a_batch(b, False)
            a_batch(NB - 1, True)

            def b_turned_x(b):
                act.wait_ge(b_hT_ps, b + 1)
                nc.scalar.activation(hT[:, :], N2[:, 0:S], ACT.Identity, bias=vcols[:, R_B:R_B + 1],
                                     scale=vcols[:, R_G:R_G + 1]).then_inc(b_hT, 1)

            def b_out(b, p, first):
                if p == 0 and not first:
                    act.wait_ge(b_y, b)
                act.wait_ge(b_pv, b * NP + (p + 1))
                nc.scalar.copy(oT2[:, p, :], OV2[:, 0:S]).then_inc(b_oT, 1)

            def b_squares(b, p):
                act.wait_ge(b_qk_ps, b * NP + (p + 1))
                nc.scalar.activation(sq[:, :, :], QK2[:, :].rearrange("p (a s) -> p a s", a=2), ACT.Square).then_inc(b_sq, 1)

            def b_norms(b, p):
                act.wait_ge(b_v_ps, b * NP + (p + 1))
                nc.scalar.copy(vpair[:, p % 4, :, :], OV2[:, S:2 * S].rearrange("p (j d) -> p j d", j=ST)).then_inc(b_v, 1)
                act.wait_ge(b_n_ps, b * NP + (p + 1))
                norm = rr[:, :, :].rearrange("p a s -> p (a s)")
                nc.scalar.activation(norm, N2[:, :], ACT.Ln, bias=eps12[:, :], scale=1.0).then_inc(b_ln, 1)
                act.wait_ge(b_ln, b * NP + (p + 1))
                nc.scalar.activation(norm, norm, ACT.Exp, scale=-0.5).then_inc(b_rr, 1)

            def b_exp_pair(b, p):
                for t in range(2):
                    h = 2 * p + t
                    act.wait_ge(b_m, b * H2 + (h + 1))
                    nc.scalar.activation(prob2[:, h % 4, 0:P], smask[:, h % 4, 0:P], ACT.Exp,
                                         bias=nmax2[:, h % 4, 0:1], scale=-1.0, accum_out=sums[:, p % 2, t, 0:1])
                    nc.scalar.activation(prob2[:, h % 4, P:3 * P], smask[:, h % 4, P:3 * P], ACT.Exp,
                                         bias=nmax2[:, h % 4, 1:2], scale=-1.0, accum_out=sums[:, p % 2, t, 1:2]
                                         ).then_inc(b_exp, 1)

            def b_rsqrt(which, n):
                act.wait_ge(b_mv[which], n)
                r = rstd3[:, which, :]
                nc.scalar.activation(r, mv3[:, which, :, 1], ACT.Ln, bias=epsln[:, :], scale=1.0).then_inc(b_lnv[which], 1)
                act.wait_ge(b_lnv[which], n)
                nc.scalar.activation(r, r, ACT.Exp, scale=-0.5).then_inc(b_rstd[which], 1)

            def b_epilogue_early(b, step):
                if step == 4:
                    act.wait_ge(b_h2T_ps, b + 1)
                    act.wait_ge(b_res, b + 1)
                    nc.scalar.activation(h2T[:, :], Y2[:, 0:S], ACT.Identity, bias=vcols[:, R_B:R_B + 1],
                                         scale=vcols[:, R_G:R_G + 1]).then_inc(b_h2T, 1)
                if step == 6:
                    act.wait_ge(b_gT_ps, b + 1)
                    nc.scalar.copy(gT[:, :], Y2[0:NE, 0:S]).then_inc(b_gT, 1)
                if step == 7:
                    act.wait_ge(b_gb, b + 1)
                    nc.scalar.copy(moe0[:, ds(b * S, S)], Y2[:, 0:S]).then_inc(b_gbs, 1)

            def b_epilogue_mid(b, step):
                if step == 3:
                    b_rsqrt(2, b + 1)
                if step == 5:
                    act.wait_ge(b_glog, b + 1)
                    nc.scalar.activation(gnorm[:, :, :], glog[:, :, :], ACT.Exp).then_inc(b_gexp, 1)

            def b_batch(b, first, last_batch):
                for p in range(NP):
                    more = p < NP - 1 or not last_batch
                    nb, np_ = (b, p + 1) if p < NP - 1 else (b + 1, 0)
                    if not first or p >= 3:
                        b_out(*((b, p - 3) if p >= 3 else (b - 1, p - 3 + NP)), first)
                    if not first:
                        b_epilogue_early(b - 1, p)
                    if more:
                        b_squares(nb, np_)
                        b_norms(nb, np_)
                    if not first:
                        b_epilogue_mid(b - 1, p)
                    if p in (0, 2) and not last_batch:
                        b_rsqrt(p // 2, b + 2)
                    b_exp_pair(b, p)
                    if p == NP - 2 and not last_batch:
                        b_turned_x(b + 1)

            act.wait_ge(s_nat, 1)
            b_rsqrt(0, 1)
            b_rsqrt(1, 1)
            b_turned_x(0)
            b_squares(0, 0)
            b_norms(0, 0)
            b_batch(0, True, False)
            with act.Fori(1, NB - 1) as b:
                b_batch(b, False, False)
            b_batch(NB - 1, False, True)
            for p in range(NP - 3, NP):
                b_out(NB - 1, p, False)
            for step in range(NP):
                b_epilogue_early(NB - 1, step)
                b_epilogue_mid(NB - 1, step)

            nc.scalar.preload_act_table_set("gelu_apprx_tanh_and_others")
            with act.Fori(0, NCH) as ch:
                for e in range(NE):
                    for c in range(FC):
                        act.wait_ge(c_h, ch * (NE * FC) + (e * FC + c + 1))
                        if c == 0:
                            act.wait_ge(c_e, ch * NE + max(e, 1))
                        nc.scalar.activation(hid[:, e % 2, c, :], HB[c][:, :], ACT.Gelu_apprx_tanh,
                                             bias=vcols[:, R_B1 + e * FC + c:R_B1 + e * FC + c + 1],
                                             scale=1.0).then_inc(c_hid, 1)

        @block.vector
        def _(dve):
            link0 = Link(dve, s_link, 0)
            for credit in (a_ydone, c_acc, c_fin):
                dve.sem_inc(credit, 1)
            nc.vector.memset(vaug[:, :, :, D1:D1 + 1], 1.0)
            nc.vector.memset(blockones[:, :], 0.0)
            link0(nc.vector.memset(kpair[:, :, :, :], 0.0))
            nc.vector.memset(blockones[0:D2, 0:D2], 1.0).then_inc(s_const, 1)
            nc.vector.memset(blockones[D2:P, D2:P], 1.0).then_inc(s_const, 1)
            dve.wait_ge(s_vcol_ps, 1)
            link0(nc.vector.tensor_copy(vcols[:, :], bank[0][:, 0:P]))
            nc.vector.scalar_tensor_tensor(qks[:, :], vcols[:, R_QS:R_QS + NP], QK_SCALE, vcols[:, R_KS:R_KS + NP],
                                           ALU.mult, ALU.mult)
            for i, r in enumerate((R_G, R_B, R_GB)):
                last = nc.vector.tensor_copy(gspread[:, i, :], vcols[:, r:r + 1].broadcast_to([P, P]))
            last.then_inc(s_spread, 1)
            dve.wait_ge(s_nat_ps, 1)
            nc.vector.tensor_copy(gnat[:, :, :], bank[1][:, 0:2 * P].rearrange("p (a d) -> p a d", a=2))
            link0(nc.vector.tensor_copy(gbnat[:, :], bank[1][:, 2 * P:2 * P + NE]))
            nc.vector.tensor_copy(gbnat[:, 0:1], gbnat[:, 0:1]).then_inc(s_nat, 1)

            def x_tile(b, i):
                return xres[:, ds((b * ST + i) * P, P)]

            def a_norm_x(b, link):
                norm_stats(link, [x_tile(b, i) for i in range(ST)])
                for i in range(ST):
                    last = normalize(xh[:, i, :], x_tile(b, i), i)
                last.then_inc(a_xh, 1)

            def a_values(b):
                dve.wait_ge(a_v_ps, b + 1)
                nc.vector.tensor_copy(vaug[:, :, :, 0:D1], VX[:, 0:S].rearrange("p (i h d) -> p i h d", i=ST, h=H1)
                                      ).then_inc(a_v, 1)

            def a_turned(b, h):
                dve.wait_ge(a_t, b * H1 + (h + 1))
                if h >= 2:
                    dve.wait_ge(a_pv, b * H1 + (h - 1))
                nc.vector.tensor_copy(probT[:, h % 2, :, :], TB[h % 2][:, :].rearrange("p (j s) -> p j s", j=ST)
                                      ).then_inc(a_pT, 1)

            def a_batch(b, link, last_batch):
                for k in range(H1 + 2):
                    if k < H1:
                        dve.wait_ge(a_s, b * H1 + (k + 1))
                        nc.vector.tensor_reduce(nmax[:, k % 4, :], SB[k % 3][:, :].rearrange("p (i t) -> p i t", i=ST),
                                                X_AXIS, ALU.max, negate=True).then_inc(a_nmax, 1)
                    if k == 1:
                        a_values(b)
                    if k >= 2:
                        a_turned(b, k - 2)
                    if k == 8 and not last_batch:
                        a_norm_x(b + 1, link)
                dve.wait_ge(a_pv, b * H1 + H1)
                link(nc.vector.reciprocal(rsum[:, :, :], O1[:, :, :, D1]))
                nc.vector.tensor_tensor(onat[:, :, :].rearrange("p i (h d) -> p i h d", h=H1), O1[:, :, :, 0:D1],
                                        rsum[:, :, :].unsqueeze(3).broadcast_to([P, ST, H1, D1]), ALU.mult
                                        ).then_inc(a_onat, 1)
                dve.wait_ge(a_y, b + 1)
                norm_stats(link, [TB[1][:, i * P:(i + 1) * P] for i in range(ST)])
                for i in range(ST):
                    last = normalize(tmp[:, i, :], TB[1][:, i * P:(i + 1) * P], i)
                link(last)
                for i in range(ST):
                    last = nc.vector.tensor_tensor(x_tile(b, i), x_tile(b, i), tmp[:, i, :], ALU.add)
                last.then_inc(a_ydone, 1)

            for i in range(XQ):
                dve.wait_ge(s_x, 16 * XQ)
            a_norm_x(0, link0)
            A_LINKS = 2 * NORM_LINKS + 2
            with dve.Fori(0, NB - 1) as b:
                link = Link(dve, a_link, b * A_LINKS)
                a_batch(b, link, False)
                assert link.n == A_LINKS, link.n
            link = Link(dve, a_link, (NB - 1) * A_LINKS)
            a_batch(NB - 1, link, True)
            dve.wait_ge(a_ydone, NB + 1)

            def b_stats(which, tiles, link):
                for i, tile in enumerate(tiles):
                    last = nc.vector.bn_stats(bst3[:, which, i, :], tile)
                link(last)
                carry_wait()
                for i in range(ST):
                    last = nc.vector.bn_aggr(mv3[:, which, i, :], bst3[:, which, i, :])
                last.then_inc(b_mv[which], 1)

            def b_norm(which, n, dst, src):
                dve.wait_ge(b_rstd[which], n)
                for i in range(ST):
                    last = nc.vector.tensor_scalar(dst[i], src[i], mv3[:, which, i, 0:1], rstd3[:, which, i:i + 1],
                                                   ALU.subtract, ALU.mult)
                return last

            xt = [tmp[:, i, :] for i in range(ST)]

            def b_norm_x(b, step, link):
                if step == 0:
                    b_stats(0, [x_tile(b, i) for i in range(ST)], link)
                if step == 1:
                    link(b_norm(0, b + 1, xt, [x_tile(b, i) for i in range(ST)]))
                if step == 2:
                    b_stats(1, xt, link)
                if step == 3:
                    b_norm(1, b + 1, [xh[:, i, :] for i in range(ST)], xt).then_inc(b_xh, 1)

            def b_normalize_qk(b, p):
                dve.wait_ge(b_rr, b * NP + (p + 1))
                nc.vector.scalar_tensor_tensor(qTs[:, p % 2, :], QK2[:, 0:S], qks[:, p:p + 1], rr[:, 0, :], ALU.mult, ALU.mult)
                for t in range(2):
                    r = slice(t * D2, (t + 1) * D2)
                    last = nc.vector.tensor_tensor(kpair[r, p % 2, t, :], QK2[r, S:2 * S], rr[r, 1, :], ALU.mult)
                last.then_inc(b_k, 1)

            def b_maxes(b, p, t):
                h = 2 * p + t
                dve.wait_ge(b_s, b * H2 + (h + 1))
                carry_wait()
                nc.vector.tensor_tensor_reduce(
                    out=smask[:, h % 4, 0:P], in0=S2[t][:, 0:P], in1=causal[:, 1, :],
                    scale=-1.0, scalar=3.0e38, op0=ALU.add, op1=ALU.min, accum_out=nmax2[:, h % 4, 0:1])
                nc.vector.tensor_tensor_reduce(
                    out=smask[:, h % 4, P:3 * P], in0=S2[t][:, P:3 * P], in1=causal[:, :, :].rearrange("p a s -> p (a s)"),
                    scale=-1.0, scalar=3.0e38, op0=ALU.add, op1=ALU.min, accum_out=nmax2[:, h % 4, 1:2]).then_inc(b_m, 1)

            def b_sums(b, p):
                dve.wait_ge(b_exp, b * H2 + 2 * (p + 1))
                nc.vector.reciprocal(rblk[:, p % 2, :, 0:2], sums[:, p % 2, :, :])
                nc.vector.reciprocal(rblk[:, p % 2, :, 2:3], sums[:, p % 2, :, 1:2]).then_inc(b_rec, 1)

            def b_turned(b, p):
                for t in range(2):
                    dve.wait_ge(b_t, b * H2 + (2 * p + t + 1))
                    nc.vector.tensor_copy(prob2T[:, p % 2, t, :], T2[t][:, 0:3 * P]).then_inc(b_pT, 1)

            def b_epilogue_early(b, step, link):
                if step == 3:
                    dve.wait_ge(b_y, b + 1)
                    b_stats(2, [Y2[:, i * P:(i + 1) * P] for i in range(ST)], link)
                if step == 5:
                    dve.wait_ge(b_gl, b + 1)
                    link(nc.vector.tensor_tensor(glog[:, :, :], Y2[:, 0:ST * NE].rearrange("p (i e) -> p i e", i=ST),
                                                 gbnat[:, :].unsqueeze(1).broadcast_to([P, ST, NE]), ALU.add))
                    link(nc.vector.tensor_reduce(gmx[:, :], glog[:, :, :], X_AXIS, ALU.max))
                    nc.vector.tensor_tensor(glog[:, :, :], glog[:, :, :],
                                            gmx[:, :].unsqueeze(2).broadcast_to([P, ST, NE]), ALU.subtract).then_inc(b_glog, 1)

            def b_epilogue_late(b, step, link):
                if step == 3:
                    b_norm(2, b + 1, [h2n[:, i, :] for i in range(ST)], [Y2[:, i * P:(i + 1) * P] for i in range(ST)]
                           ).then_inc(b_h2n, 1)
                if step == 5:
                    dve.wait_ge(b_gexp, b + 1)
                    link(nc.vector.tensor_reduce(gsm[:, :], gnorm[:, :, :], X_AXIS, ALU.add))
                    link(nc.vector.reciprocal(gmx[:, :], gsm[:, :]))
                    link(nc.vector.tensor_tensor(gnorm[:, :, :], gnorm[:, :, :],
                                                 gmx[:, :].unsqueeze(2).broadcast_to([P, ST, NE]), ALU.mult))
                    nc.vector.tensor_copy(gates[:, ds(b * (ST * NE), ST * NE)],
                                          gnorm[:, :, :].rearrange("p i e -> p (i e)")).then_inc(b_gate, 1)

            def b_batch(b, link, first, last_batch):
                for p in range(NP):
                    more = p < NP - 1 or not last_batch
                    nb, np_ = (b, p + 1) if p < NP - 1 else (b + 1, 0)
                    pb, pp = (b, p - 1) if p >= 1 else (b - 1, NP - 1)
                    if not first:
                        b_epilogue_early(b - 1, p, link)
                    if p in (0, 2) and not last_batch:
                        b_norm_x(b + 1, p, link)
                    if not first or p >= 1:
                        b_sums(pb, pp)
                    b_maxes(b, p, 0)
                    b_maxes(b, p, 1)
                    if more:
                        b_normalize_qk(nb, np_)
                    if not first or p >= 1:
                        b_turned(pb, pp)
                    if not first:
                        b_epilogue_late(b - 1, p, link)
                    if p in (1, 4) and not last_batch:
                        b_norm_x(b + 1, 1 if p == 1 else 3, link)

            for step in range(4):
                b_norm_x(0, step, link0)
            b_normalize_qk(0, 0)
            n_first = 3
            B_LINKS = n_first + 1 + 5
            link = Link(dve, b_link, 0)
            b_batch(0, link, True, False)
            assert link.n == n_first, link.n
            with dve.Fori(1, NB - 1) as b:
                link = Link(dve, b_link, (b - 1) * B_LINKS + n_first)
                b_batch(b, link, False, False)
                assert link.n == B_LINKS, (link.n, B_LINKS)
            link = Link(dve, b_link, (NB - 2) * B_LINKS + n_first)
            b_batch(NB - 1, link, False, True)
            b_sums(NB - 1, NP - 1)
            b_turned(NB - 1, NP - 1)
            for step in range(NP):
                b_epilogue_early(NB - 1, step, link)
                b_epilogue_late(NB - 1, step, link)

            dve.wait_ge(b_gbs, NB + 1)
            dve.wait_ge(b_gate, NB)

            def c_chunk(ch, half, link):
                dve.wait_ge(c_fin, ch + 1)
                nc.vector.tensor_copy(gch[:, :, :], gates[:, ds(ch * (CT * NE), CT * NE)].rearrange("p (i e) -> p i e", i=CT))
                link(nc.vector.tensor_copy(acc[:, :, :], moe0[:, ds(ch * CW, CW)].rearrange("p (i d) -> p i d", i=CT)))
                for e in range(NE):
                    dve.wait_ge(c_e, ch * NE + (e + 2))
                    for i in range(CT):
                        last = nc.vector.scalar_tensor_tensor(acc[:, i, :], EB[e % 2][:, i * P:(i + 1) * P],
                                                              gch[:, i, e:e + 1], acc[:, i, :], ALU.mult, ALU.add)
                    last.then_inc(c_acc, 1)
                    dve.wait_ge(c_acc, ch * NE + (e + 2))
                norm_stats(link, [acc[:, i, :] for i in range(CT)])
                for i in range(CT):
                    last = normalize(tmp[:, i, :], acc[:, i, :], i)
                link(last)
                link(nc.vector.tensor_tensor(acc[:, :, :], tmp[:, :, :],
                                             gnat[:, 0:1, :].broadcast_to([P, CT, P]), ALU.mult))
                link(nc.vector.tensor_tensor(tmp[:, :, :], acc[:, :, :],
                                             gnat[:, 1:2, :].broadcast_to([P, CT, P]), ALU.add))
                norm_stats(link, [tmp[:, i, :] for i in range(CT)])
                for i in range(CT):
                    last = normalize(acc[:, i, :], tmp[:, i, :], i)
                link(last)
                return nc.vector.tensor_tensor(fin[:, half, :, :], acc[:, :, :],
                                               xres[:, ds(ch * CW, CW)].rearrange("p (i d) -> p i d", i=CT), ALU.add)

            C_LINKS = 2 * NORM_LINKS + 5
            with dve.Fori(0, NCH // 2) as ii:
                link = Link(dve, c_link, ii * (2 * C_LINKS))
                for j in range(2):
                    if j == 0:
                        dve.wait_ge(s_out, ii * 32 + 16)
                    c_chunk(ii * 2 + j, j, link).then_inc(c_fin, 1)
                assert link.n == 2 * C_LINKS, link.n


_INS = ['L0_attn_x', 'L0_attn_w_qkv', 'L0_attn_w_out', 'L0_ffn_ln_g', 'L0_ffn_ln_b', 'L0_ffn_Wq', 'L0_ffn_Wk', 'L0_ffn_Wv',
        'L0_ffn_q_scale', 'L0_ffn_k_scale', 'L0_ffn_Wo', 'L0_ffn_gate_w', 'L0_ffn_gate_b', 'L0_ffn_w1', 'L0_ffn_b1',
        'L0_ffn_w2', 'L0_ffn_b2']


def kernel(**inputs):
    import numpy as _np
    import concourse.bacc as _bacc
    from concourse import mybir as _mybir
    from concourse.bass_utils import run_bass_kernel_spmd as _run

    nc = _bacc.Bacc("TRN2", target_bir_lowering=False, num_devices=1)
    arrays, args = {}, []
    for name in _INS:
        a = _np.ascontiguousarray(inputs[name])
        arrays[f"in_{name}"] = a
        args.append(nc.dram_tensor(f"in_{name}", a.shape, _mybir.dt.from_np(a.dtype), kind="ExternalInput").ap())
    shape = inputs['L0_attn_x'].shape
    args.append(nc.dram_tensor("out_0", shape, _mybir.dt.float32, kind="ExternalOutput").ap())
    sandwich_kernel(nc, *args)
    r = _run(nc, [arrays], core_ids=[0])
    return r.results[0]["out_0"]
```

```python
from contextlib import ExitStack

import concourse.bass as bass
from concourse import mybir

F32 = mybir.dt.float32
BF16 = mybir.dt.bfloat16
I32 = mybir.dt.int32
ALU = mybir.AluOpType
ACT = mybir.ActivationFunctionType
X_AXIS = mybir.AxisListType.X

P = 128
LN_EPS = 1e-5
L2_EPS = 1e-12
QK_SCALE = 10.0
MASKED = -1.0e30
RSQRT_MAGIC = float(0x5F3759DF)
NORM_LINKS = 14
PART_PAIRS = ((0, 0), (1, 1), (0, 1), (1, 0), (0, 2), (2, 0))


def ds(start, size):
    return bass.ds(start, size)


class Link:

    def __init__(self, engine, sem, base):
        self.engine, self.sem, self.base, self.n = engine, sem, base, 0

    def __call__(self, instruction):
        self.n += 1
        instruction.then_inc(self.sem, 1)
        self.engine.wait_ge(self.sem, self.base + self.n)


def sandwich_kernel(nc, x, w_qkv, w_out, ln_g, ln_b, Wq, Wk, Wv, q_scale, k_scale, Wo, gate_w, gate_b,
                    w1, b1, w2, b2, out):
    NB, S, E = x.shape
    ST = S // P
    NT = NB * ST
    H1 = 16
    D1 = E // H1
    H2, _, D2 = q_scale.shape
    NP = H2 * D2 // P
    NE, _, FF = w1.shape
    FC = FF // P
    assert E == P and ST == 2 and D2 * 2 == P and H2 == 2 * NP
    CT = 4
    NCH = NT // CT
    CW = CT * P

    ctx = ExitStack()
    with ctx:
        def sb(name, shape, dt=F32):
            return ctx.enter_context(nc.sbuf_tensor(name, shape, dt))

        def sem(name):
            return ctx.enter_context(nc.semaphore(name))

        bank = [ctx.enter_context(nc.psum_tensor(f"bank{i}", [P, 512], F32)) for i in range(8)]

        xres = sb("xres", [P, NT * P])
        hTres = sb("hTres", [P, NT * P])
        gates = sb("gates", [P, NT * NE])
        wqkv_sb = sb("wqkv_sb", [P, 3 * E])
        wout_sb = sb("wout_sb", [P, E])
        wq_sb = sb("wq_sb", [P, H2 * D2])
        wk_sb = sb("wk_sb", [P, H2 * D2])
        wv_sb = sb("wv_sb", [P, H2 * D2])
        wo_sb = sb("wo_sb", [P, NP, E])
        gw_sb = sb("gw_sb", [P, NE])
        w1_sb = sb("w1_sb", [P, NE, FF])
        w2_sb = sb("w2_sb", [P, NE * FC, E])
        b2_sb = sb("b2_sb", [P, E])
        R_B1, R_QS, R_KS, R_G, R_B, R_GB = 0, NE * FC, NE * FC + NP, NE * FC + 2 * NP, NE * FC + 2 * NP + 1, NE * FC + 2 * NP + 2
        vrows = sb("vrows", [P, P])
        vcols = sb("vcols", [P, P])
        qks = sb("qks", [P, NP])
        gspread = sb("gspread", [P, 3, P])
        gnat = sb("gnat", [P, 2, P])
        gbnat = sb("gbnat", [P, NE])
        ident = sb("ident", [P, P])
        causal = sb("causal", [P, 2, P])
        blockones = sb("blockones", [P, P])
        eps12 = sb("eps12", [P, 1])

        bst = sb("bst", [P, CT, 6])
        mv = sb("mv", [P, CT, 2])
        pad = sb("pad", [P, 64])
        bst3 = sb("bst3", [P, 3, ST, 6])
        mv3 = sb("mv3", [P, 3, ST, 2])
        rstd3 = sb("rstd3", [P, 3, ST])
        epsln = sb("epsln", [P, 1])
        rs_v = sb("rs_v", [P, CT])
        rs_t = sb("rs_t", [P, CT], I32)
        rs_i = sb("rs_i", [P, CT], I32)
        rs_a = sb("rs_a", [P, CT])
        rs_y = sb("rs_y", [P, CT])

        xh = sb("xh", [P, ST, P])
        xT = sb("xT", [P, S])
        parts = sb("parts", [P, 3, 2 * S], BF16)
        rest = sb("rest", [P, 2 * S])
        one = sb("one", [P, 1])
        KROWS = 96
        NPAIR = len(PART_PAIRS)
        STK = 2 * H1 * S
        work = sb("work", [P, STK])
        stk = work[:, :].bitcast(BF16)
        vpair = work[:, STK // 2:STK // 4 * 3].rearrange("p (a i c) -> p a i c", a=8, i=ST)
        oT2 = work[:, STK // 4 * 3:].rearrange("p (a s) -> p a s", s=S)
        GH = 4
        VW = P // GH
        vaug = sb("vaug", [P, ST, H1, VW])
        nmax = sb("nmax", [P, 4, ST])
        prob = sb("prob", [P, 4, ST, S])
        probT = hTres[:, :].rearrange("p (h j s) -> p h j s", h=2 * GH, j=ST)
        og = sb("og", [P, S])
        rsum = sb("rsum", [P, ST, GH])
        onat = sb("onat", [P, ST, P])
        oT = sb("oT", [P, S])
        tmp = sb("tmp", [P, CT, P])

        hT = sb("hT", [P, S])
        qTs = sb("qTs", [P, 2, S])
        sq = sb("sq", [P, 2, S])
        rr = sb("rr", [P, 2, 2, S])
        kpair = sb("kpair", [P, 2, 2, S])
        smask = sb("smask", [P, 4, 3 * P])
        nmax2 = sb("nmax2", [P, 4, ST])
        prob2 = sb("prob2", [P, 4, 3 * P])
        prob2T = sb("prob2T", [P, 2, 2, 3 * P])
        sums = sb("sums", [P, 2, 2, ST])
        rblk = sb("rblk", [P, 2, 2, 3])
        h2n = sb("h2n", [P, ST, P])
        h2T = sb("h2T", [P, S])
        glog = sb("glog", [P, ST, NE])
        gmx = sb("gmx", [P, ST])
        gsm = sb("gsm", [P, ST])
        gnorm = sb("gnorm", [P, ST, NE])

        hid = work[:, 0:2 * FC * CW].rearrange("p (a c t) -> p a c t", a=2, c=FC)
        acc = sb("acc", [P, CT, P])
        gch = sb("gch", [P, CT, NE])
        gT = sb("gT", [P, CW])
        fin = sb("fin", [P, 2, CT, P])

        s_x, s_wa, s_wb, s_wc, s_vec, s_out = (sem(n) for n in ("s_x", "s_wa", "s_wb", "s_wc", "s_vec", "s_out"))
        s_vz, s_const, s_zero, s_vcol_ps, s_vcols, s_spread, s_nat_ps, s_nat = (
            sem(n) for n in ("s_vz", "s_const", "s_zero", "s_vcol_ps", "s_vcols", "s_spread", "s_nat_ps", "s_nat"))
        s_cst1 = sem("s_cst1")
        s_x0 = sem("s_x0")
        s_link = sem("s_link")
        a_xh, a_xT_ps, a_xT, a_qk_ps, a_v_ps, a_hi, a_rest, a_mid, a_parts, a_scr, a_stk, a_v = (
            sem("a_" + n) for n in ("xh", "xT_ps", "xT", "qk_ps", "v_ps", "hi", "rest", "mid", "parts", "scr", "stk", "v"))
        a_pTs = sem("a_pTs")
        qk_dram = nc.dram_tensor("qk_parts", [2, 3, P, 2 * S], BF16, kind="Internal").ap()
        a_s, a_nmax, a_exp, a_t, a_pT, a_pv, a_og, a_on_ps, a_onat, a_oT_ps, a_oT, a_y, a_ydone, a_link = (
            sem("a_" + n) for n in ("s", "nmax", "exp", "t", "pT", "pv", "og", "on_ps", "onat", "oT_ps", "oT", "y", "ydone", "link"))
        a_mv, a_lnv, a_rstd = ({i: sem(f"a_{n}{i}") for i in (0, 2)} for n in ("mv", "lnv", "rstd"))
        b_xh, b_hT_ps, b_hT, b_qk_ps, b_sq, b_n_ps, b_ln, b_rr, b_k, b_v_ps, b_v = (
            sem("b_" + n) for n in ("xh", "hT_ps", "hT", "qk_ps", "sq", "n_ps", "ln", "rr", "k", "v_ps", "v"))
        b_s, b_m, b_exp, b_rec, b_pn, b_t, b_pT, b_pv, b_oT, b_y, b_link = (
            sem("b_" + n) for n in ("s", "m", "exp", "rec", "pn", "t", "pT", "pv", "oT", "y", "link"))
        b_mv, b_lnv, b_rstd = ([sem(f"b_{n}{i}") for i in range(3)] for n in ("mv", "lnv", "rstd"))
        b_h2n, b_h2T_ps, b_h2T, b_gl, b_glog, b_gexp, b_gate, b_res = (
            sem("b_" + n) for n in ("h2n", "h2T_ps", "h2T", "gl", "glog", "gexp", "gate", "res"))
        c_h, c_hid, c_e, c_acc, c_g, c_gT_ps, c_gT, c_gb, c_link, c_fin = (
            sem("c_" + n) for n in ("h", "hid", "e", "acc", "g", "gT_ps", "gT", "gb", "link", "fin"))

        block = ctx.enter_context(nc.Block())

        XQ = 4
        STACKED = 16 * 2 * NPAIR
        x_rows = x.rearrange("b (i p) e -> p (b i) e", p=P)
        out_rows = out.rearrange("b (i p) e -> p (b i) e", p=P)
        xres_t = xres[:, :].rearrange("p (t e) -> p t e", e=P)

        @block.sync
        def _(sp):
            sp.wait_ge(s_vz, 3)
            n = NT // XQ
            sp.dma_start(xres_t[:, 0:n, :], x_rows[:, 0:n, :]).then_inc(s_x0, 16)
            sp.dma_start(wqkv_sb[:, :], w_qkv).then_inc(s_wa, 16)
            sp.dma_start(wout_sb[:, :], w_out).then_inc(s_wa, 16)
            for i in range(1, XQ):
                sp.dma_start(xres_t[:, i * n:(i + 1) * n, :], x_rows[:, i * n:(i + 1) * n, :]).then_inc(s_x, 16)
            sp.dma_start(vrows[R_B1:R_B1 + NE * FC, :], b1.rearrange("e (c f) -> (e c) f", f=P)).then_inc(s_vec, 16)
            sp.dma_start(vrows[R_QS:R_QS + NP, :], q_scale.rearrange("(p t) o d -> p (t o d)", t=2)).then_inc(s_vec, 16)
            sp.dma_start(vrows[R_KS:R_KS + NP, :], k_scale.rearrange("(p t) o d -> p (t o d)", t=2)).then_inc(s_vec, 16)
            sp.dma_start(vrows[R_G:R_G + 1, :], ln_g.rearrange("(a d) -> a d", a=1)).then_inc(s_vec, 16)
            sp.dma_start(vrows[R_B:R_B + 1, :], ln_b.rearrange("(a d) -> a d", a=1)).then_inc(s_vec, 16)
            sp.dma_start(vrows[R_GB:R_GB + 1, 0:NE], gate_b.rearrange("(a d) -> a d", a=1)).then_inc(s_vec, 16)

            def stack(n, j, first):
                sp.wait_ge(a_parts, n + 1)
                sp.dma_start(qk_dram[j].rearrange("r p s -> p r s"), parts[:, :, :]).then_inc(a_scr, 16)
                if first:
                    sp.wait_ge(s_zero, j + 1)
                sp.wait_ge(a_scr, n * 16 + 16)
                both = stk[:, j * STK:(j + 1) * STK].rearrange("p (a h s) -> p a h s", a=2, h=H1)
                for r, pair in enumerate(PART_PAIRS):
                    for a in range(2):
                        src = qk_dram[j, pair[a], :, a * S:(a + 1) * S].rearrange("(h d) s -> d h s", d=D1)
                        sp.dma_start(both[r * D1:(r + 1) * D1, a, :, :], src).then_inc(a_stk, 16)

            for j in range(2):
                stack(j, j, True)
            for w_sb, w in ((wq_sb[:, :], Wq), (wk_sb[:, :], Wk), (wv_sb[:, :], Wv), (gw_sb[:, :], gate_w),
                            (b2_sb[0:NE, :], b2)):
                sp.dma_start(w_sb, w).then_inc(s_wb, 16)
            sp.dma_start(wo_sb[:, :, :], Wo.rearrange("(k p) e -> p k e", p=P)).then_inc(s_wb, 16)
            sp.dma_start(w1_sb[:, :, :], w1.rearrange("e d f -> d e f")).then_inc(s_wc, 16)
            sp.dma_start(w2_sb[:, :, :], w2.rearrange("e (c f) d -> f (e c) d", f=P)).then_inc(s_wc, 16)
            with sp.Fori(1, NB // 2) as ii:
                for j in range(2):
                    stack(ii * 2 + j, j, False)
            sp.sem_inc(s_out, 16)
            with sp.Fori(0, NCH // 2) as ii:
                for j in range(2):
                    sp.wait_ge(c_fin, ii * 2 + (j + 2))
                    sp.dma_start(out_rows[:, ds(ii * (2 * CT) + j * CT, CT), :], fin[:, j, :, :]).then_inc(s_out, 16)
            sp.wait_ge(s_out, 16 * (NCH + 1))

        @block.gpsimd
        def _(pool):
            pool.sem_inc(b_res, 1)
            nc.gpsimd.memset(vrows[:, :], 0.0).then_inc(s_vz, 1)
            nc.gpsimd.memset(b2_sb[:, :], 0.0).then_inc(s_vz, 1)
            nc.gpsimd.memset(gT[:, :], 0.0).then_inc(s_vz, 1)
            nc.gpsimd.memset(ident[:, :], 0.0).then_inc(s_cst1, 1)
            nc.gpsimd.memset(causal[:, :, :], 0.0).then_inc(s_cst1, 1)
            nc.gpsimd.memset(eps12[:, :], L2_EPS).then_inc(s_const, 1)
            nc.gpsimd.memset(epsln[:, :], LN_EPS).then_inc(s_const, 1)
            pool.wait_ge(s_cst1, 2)
            nc.gpsimd.affine_select(out=ident[:, :], in_=ident[:, :], compare_op=ALU.not_equal, fill=1.0,
                                    base=0, pattern=[[-1, P]], channel_multiplier=1).then_inc(s_const, 1)
            nc.gpsimd.affine_select(out=causal[:, 1, :], in_=causal[:, 1, :], compare_op=ALU.is_ge, fill=MASKED,
                                    base=0, pattern=[[-1, P]], channel_multiplier=1).then_inc(s_const, 1)

            nc.gpsimd.memset(one[:, :], 1.0).then_inc(s_cst1, 1)
            pool.wait_ge(s_cst1, 3)
            for j in range(2):
                nc.gpsimd.memset(work[:, j * STK // 2:(j + 1) * STK // 2], 0.0).then_inc(s_zero, 1)
            pool.wait_ge(s_zero, 2)

            def split(n, first):
                pool.wait_ge(a_rest, n + 1)
                nc.gpsimd.tensor_tensor(parts[:, 1, :], rest[:, :],
                                        one[:, :].broadcast_to([P, 2 * S]), ALU.mult).then_inc(a_mid, 1)
                pool.wait_ge(a_mid, n + 1)
                if not first or n > 0:
                    pool.wait_ge(a_stk, n * STACKED)
                if not first:
                    pool.wait_ge(a_s, (n - 1) * H1)
                nc.gpsimd.tensor_tensor(parts[:, 2, :], rest[:, :], parts[:, 1, :], ALU.subtract).then_inc(a_parts, 1)

            for n in range(2):
                split(n, True)
            with pool.Fori(2, NB) as n:
                split(n, False)

            def b_normalize(b, p, keep):
                for t in range(2):
                    h = 2 * p + t
                    pool.wait_ge(b_rec, b * H2 + (h + 1))
                    pr = prob2[:, h % 4, :].rearrange("q (n s) -> q n s", n=3)
                    nc.gpsimd.tensor_tensor(pr, pr, rblk[:, p % 2, t, :].unsqueeze(2).broadcast_to([P, 3, P]),
                                            ALU.mult).then_inc(b_pn, 1)
                    if keep and p == 5 and t == 0:
                        b_keep_input(b - 1)

            def b_keep_input(b):
                pool.wait_ge(b_h2T, b + 1)
                nc.gpsimd.tensor_copy(hTres[:, ds(b * S, S)], h2T[:, :]).then_inc(b_res, 1)

            for p in range(NP):
                b_normalize(0, p, False)
            with pool.Fori(1, NB) as b:
                for p in range(NP):
                    b_normalize(b, p, True)
            b_keep_input(NB - 1)

        carried = [0]

        def carry_wait():
            carried[0] += 1
            nc.vector.memset(pad[:, carried[0] % 64:carried[0] % 64 + 1], 0.0)

        def rsqrt_steps(link, n, var, eps):
            v, t, i, a, y = (q[:, 0:n] for q in (rs_v, rs_t, rs_i, rs_a, rs_y))
            link(nc.vector.tensor_scalar_add(v, var, eps))
            link(nc.vector.tensor_single_scalar(t, v.bitcast(I32), 1, ALU.arith_shift_right))
            link(nc.vector.tensor_scalar(i, t, -1.0, RSQRT_MAGIC, ALU.mult, ALU.add))
            guess = i.bitcast(F32)
            for step in range(3):
                yy = guess if step == 0 else y
                link(nc.vector.tensor_tensor(a, yy, yy, ALU.mult))
                link(nc.vector.scalar_tensor_tensor(a, a, -0.5, v, ALU.mult, ALU.mult))
                link(nc.vector.scalar_tensor_tensor(y, a, 1.5, yy, ALU.add, ALU.mult))

        def norm_stats(link, tiles):
            n = len(tiles)
            for i, tile in enumerate(tiles):
                last = nc.vector.bn_stats(bst[:, i, :], tile)
            link(last)
            carry_wait()
            for i in range(n):
                last = nc.vector.bn_aggr(mv[:, i, :], bst[:, i, :])
            link(last)
            rsqrt_steps(link, n, mv[:, 0:n, 1], LN_EPS)

        def normalize(dst, src, i):
            return nc.vector.tensor_scalar(dst, src, mv[:, i, 0:1], rs_y[:, i:i + 1], ALU.subtract, ALU.mult)

        SB, TB = bank[0:3], bank[3:5]
        QK, VX, OB = bank[5], bank[6], bank[7]
        OG, ON = OB[:, 0:S], OB[:, S:2 * S]
        YT, Y1 = QK[:, 0:S], QK[:, S:2 * S]
        NG = H1 // GH
        S2, T2, QK2 = bank[0:2], bank[3], bank[4:6]
        N2, OV2, Y2 = bank[6], bank[7], bank[2]
        HB, EB, GT, GB = bank[0:4], bank[4:6], bank[6], bank[7]

        BLOCKS = ((0, 0), (1, 0), (1, 1))

        @block.tensor
        def _(pe):
            pe.sem_inc(c_e, 1)
            pe.wait_ge(s_const, 6)
            pe.wait_ge(s_wa, 32)

            def a_turn_x(b):
                pe.wait_ge(a_xh, b + 2)
                for i in range(ST):
                    last = nc.tensor.transpose(VX[:, (ST + i) * P:(ST + i + 1) * P], xh[:, i, :], ident[:, :])
                last.then_inc(a_xT_ps, 1)

            def a_project_qk(n, start):
                pe.wait_ge(a_xT, n + 1)
                if start and n > 0:
                    pe.wait_ge(a_rest, n)
                nc.tensor.matmul(QK[:, 0:S], wqkv_sb[:, 0:E], xT[:, :], start=True, stop=True)
                nc.tensor.matmul(QK[:, S:2 * S], wqkv_sb[:, E:2 * E], xT[:, :], start=True, stop=True).then_inc(a_qk_ps, 1)

            def a_project_v(n):
                for i in range(ST):
                    last = nc.tensor.matmul(VX[:, i * P:(i + 1) * P], xT[:, i * P:(i + 1) * P],
                                            wqkv_sb[:, 2 * E:3 * E], start=True, stop=True)
                last.then_inc(a_v_ps, 1)

            def head_back(b, k, n, size=H1):
                return (b, k - n) if k >= n else (b - 1, k - n + size)

            def a_scores(b, k, first):
                if k == 0:
                    pe.wait_ge(a_stk, b * STACKED + STACKED)
                if k == 0 and not first:
                    pe.wait_ge(a_exp, b * H1)
                elif k >= 3:
                    pe.wait_ge(a_exp, b * H1 + (k - 2))
                for i in range(ST):
                    q_at = (b % 2) * STK + (k * S + i * P)
                    k_at = (b % 2) * STK + (H1 + k) * S
                    last = nc.tensor.matmul(SB[k % 3][:, i * S:(i + 1) * S], stk[0:KROWS, ds(q_at, P)],
                                            stk[0:KROWS, ds(k_at, S)], start=True, stop=True)
                last.then_inc(a_s, 1)

            def a_turn_probs(b, h, first):
                pe.wait_ge(a_exp, b * H1 + (h + 1))
                if h >= 2 or not first:
                    pe.wait_ge((a_pT, a_pTs)[h % 2], b * (H1 // 2) + h // 2)
                for j in range(ST):
                    for i in range(ST):
                        last = nc.tensor.transpose(TB[h % 2][:, j * S + i * P:j * S + (i + 1) * P],
                                                   prob[:, h % 4, i, j * P:(j + 1) * P], ident[:, :])
                last.then_inc(a_t, 1)

            def a_values(b, g, first):
                if g == 0:
                    pe.wait_ge(a_v, b + 1)
                if g >= 1 or not first:
                    pe.wait_ge(a_onat, b * NG + g)
                pe.wait_ge(a_pT, b * (H1 // 2) + (g + 1) * (GH // 2))
                pe.wait_ge(a_pTs, b * (H1 // 2) + (g + 1) * (GH // 2))
                for j in range(ST):
                    for t in range(GH):
                        h = g * GH + t
                        last = nc.tensor.matmul(OG[t * VW:(t + 1) * VW, :], vaug[:, j, h, :], probT[:, h % (2 * GH), j, :],
                                                start=(j == 0), stop=(j == ST - 1))
                last.then_inc(a_pv, 1)

            def a_turn_outputs(b, g):
                pe.wait_ge(a_og, b * NG + (g + 1))
                for i in range(ST):
                    last = nc.tensor.transpose(ON[:, i * P:(i + 1) * P], og[:, i * P:(i + 1) * P], ident[:, :])
                last.then_inc(a_on_ps, 1)

            def a_epilogue(b, k, qk_left):
                if k == 8:
                    pe.wait_ge(a_onat, (b + 1) * NG)
                    pe.wait_ge(a_rest, qk_left)
                    for i in range(ST):
                        last = nc.tensor.transpose(YT[:, i * P:(i + 1) * P], onat[:, i, :], ident[:, :])
                    last.then_inc(a_oT_ps, 1)
                if k == 9:
                    pe.wait_ge(a_oT, b + 1)
                    for i in range(ST):
                        last = nc.tensor.matmul(Y1[:, i * P:(i + 1) * P], oT[:, i * P:(i + 1) * P], wout_sb[:, :],
                                                start=True, stop=True)
                    last.then_inc(a_y, 1)

            def a_lagging(b, k, first):
                if k % GH == 0 and (k > 4 or not first):
                    a_values(*head_back(b, k // GH, 2, NG), first and k == 8)
                if k % GH == 2 and (k > 6 or not first):
                    a_turn_outputs(*head_back(b, k // GH, 2, NG))

            def a_batch(b, first, ahead, last_batch):
                for k in range(H1):
                    if k > 0 or first:
                        a_scores(b, k, first)
                    if k >= 3 or not first:
                        a_turn_probs(*head_back(b, k, 3), first and k < 5)
                    if k == 0 and not first:
                        a_scores(b, k, first)
                    a_lagging(b, k, first)
                    if not first:
                        a_epilogue(b - 1, k, NB if last_batch else b + 2)
                    if k == 7 and not last_batch:
                        pe.wait_ge(a_v, b + 1)
                        a_project_v(b + 1)
                    if ahead and k == 10:
                        a_turn_x(b + 2)
                    if ahead and k == 14:
                        if not first:
                            pe.wait_ge(a_ydone, b + 1)
                        else:
                            pe.wait_ge(a_rest, 2)
                        a_project_qk(b + 2, False)

            for n in range(2):
                a_turn_x(n)
                a_project_qk(n, True)
                if n == 0:
                    a_project_v(0)
            pe.wait_ge(s_vec, 16 * 6)
            nc.tensor.transpose(bank[0][:, 0:P], vrows[:, :], ident[:, :]).then_inc(s_vcol_ps, 1)
            pe.wait_ge(s_spread, 1)
            for i in range(3):
                last = nc.tensor.transpose(bank[1][:, i * P:(i + 1) * P], gspread[:, i, :], ident[:, :])
            last.then_inc(s_nat_ps, 1)
            pe.wait_ge(s_nat, 1)
            a_batch(0, True, True, False)
            with pe.Fori(1, NB - 2) as b:
                a_batch(b, False, True, False)
            a_batch(NB - 2, False, False, False)
            a_batch(NB - 1, False, False, True)
            for k in range(10):
                if k < 3:
                    a_turn_probs(NB - 1, H1 - 3 + k, False)
                if k <= GH + 2:
                    a_lagging(NB, k, False)
                a_epilogue(NB - 1, k, NB)

            pe.wait_ge(s_wb, 16 * 6)

            def b_turn_x(b, start):
                pe.wait_ge(b_xh, b + 1)
                if not start:
                    pe.wait_ge(b_ln, b * NP - 1)
                for i in range(ST):
                    last = nc.tensor.transpose(N2[:, i * P:(i + 1) * P], xh[:, i, :], ident[:, :])
                last.then_inc(b_hT_ps, 1)

            def b_project_qk(b, p):
                if p == 0:
                    pe.wait_ge(b_hT, b + 1)
                if not isinstance(b, int) or b * NP + p > 1:
                    pe.wait_ge(b_k, b * NP + (p - 1))
                w = slice(p * P, (p + 1) * P)
                nc.tensor.matmul(QK2[p % 2][:, 0:S], wq_sb[:, w], hT[:, :], start=True, stop=True)
                nc.tensor.matmul(QK2[p % 2][:, S:2 * S], wk_sb[:, w], hT[:, :], start=True, stop=True).then_inc(b_qk_ps, 1)

            def b_project_v(b, p, early):
                if not early:
                    pe.wait_ge(b_oT, b * NP + (p - 4))
                if early and p >= 2:
                    pe.wait_ge(b_v, p)
                for i in range(ST):
                    last = nc.tensor.matmul(OV2[:, S + i * P:S + (i + 1) * P], hT[:, i * P:(i + 1) * P],
                                            wv_sb[:, p * P:(p + 1) * P], start=True, stop=True)
                last.then_inc(b_v_ps, 1)

            def b_norms(b, p, start, after_x):
                if after_x:
                    pe.wait_ge(b_hT, b + 2)
                pe.wait_ge(b_sq, b * NP + (p + 1))
                if not start:
                    pe.wait_ge(b_ln, b * NP + p)
                nc.tensor.matmul(N2[:, :], blockones[:, :], sq[:, :, :].rearrange("p a s -> p (a s)"),
                                 start=True, stop=True).then_inc(b_n_ps, 1)

            def b_scores(b, p, t, first):
                h = 2 * p + t
                if t == 0:
                    pe.wait_ge(b_k, b * NP + (p + 1))
                if h >= 2 or not first:
                    pe.wait_ge(b_m, b * H2 + (h - 1))
                nc.tensor.matmul(S2[t][:, 0:P], qTs[:, p % 2, 0:P], kpair[:, p % 2, t, 0:P], start=True, stop=True)
                nc.tensor.matmul(S2[t][:, P:3 * P], qTs[:, p % 2, P:2 * P], kpair[:, p % 2, t, :],
                                 start=True, stop=True).then_inc(b_s, 1)

            def b_turn_probs(b, p, t, start):
                h = 2 * p + t
                pe.wait_ge(b_pn, b * H2 + (h + 1))
                if not start:
                    pe.wait_ge(b_pT, b * H2 + h)
                for n in range(3):
                    last = nc.tensor.transpose(T2[:, n * P:(n + 1) * P], prob2[:, h % 4, n * P:(n + 1) * P], ident[:, :])
                last.then_inc(b_t, 1)

            def b_values(b, p, first):
                if not first:
                    pe.wait_ge(b_oT, b * NP + p)
                pe.wait_ge(b_pT, b * H2 + 2 * (p + 1))
                for j in range(ST):
                    for t in range(2):
                        last = nc.tensor.matmul(OV2[t * D2:(t + 1) * D2, j * P:S], vpair[:, p % 8, j, t * D2:(t + 1) * D2],
                                                prob2T[:, p % 2, t, 2 * j * P:(2 + j) * P], start=(j == 0), stop=(j == 1))
                last.then_inc(b_pv, 1)

            YN = Y2[:, 0:S]

            def b_epilogue(b, step):
                if step == 2:
                    pe.wait_ge(b_oT, b * NP + NP)
                    pe.wait_ge(b_glog, b + 1)
                    for i in range(ST):
                        for p in range(NP):
                            last = nc.tensor.matmul(YN[:, i * P:(i + 1) * P], oT2[:, p, i * P:(i + 1) * P], wo_sb[:, p, :],
                                                    start=(p == 0), stop=(p == NP - 1))
                    last.then_inc(b_y, 1)
                if step == 4:
                    pe.wait_ge(b_h2n, b + 1)
                    for i in range(ST):
                        last = nc.tensor.transpose(YN[:, i * P:(i + 1) * P], h2n[:, i, :], ident[:, :])
                    last.then_inc(b_h2T_ps, 1)
                if step == 5:
                    pe.wait_ge(b_h2T, b + 1)
                    for i in range(ST):
                        last = nc.tensor.matmul(YN[:, i * NE:(i + 1) * NE], h2T[:, i * P:(i + 1) * P], gw_sb[:, :],
                                                start=True, stop=True)
                    last.then_inc(b_gl, 1)

            def back(b, p, n):
                return (b, p - n) if p >= n else (b - 1, p - n + NP)

            def ahead_of(b, p, n):
                return (b, p + n) if p + n < NP else (b + 1, p + n - NP)

            def b_batch(b, first, last_batch):
                for p in range(NP):
                    more = p < NP - 1 or not last_batch
                    nb, np_ = (b, p + 1) if p < NP - 1 else (b + 1, 0)
                    turn = not first or p >= 1
                    ahead = p < NP - 2 or not last_batch
                    ab, ap = ahead_of(b, p, 2)
                    if more:
                        b_norms(nb, np_, False, p == NP - 2 and not last_batch)
                    b_scores(b, p, 0, first)
                    if turn:
                        b_turn_probs(*back(b, p, 1), 0, first and p == 1)
                    if ahead:
                        b_project_v(ab, ap, first and p < 3)
                    if ahead:
                        b_project_qk(ab, ap)
                    b_scores(b, p, 1, first)
                    if p == NP - 3 and not last_batch:
                        b_turn_x(b + 1, False)
                    if not first or p >= 2:
                        if ahead:
                            pe.wait_ge(b_v, ab * NP + (ap + 1))
                        b_values(*back(b, p, 2), first and p == 2)
                    if turn:
                        b_turn_probs(*back(b, p, 1), 1, False)
                    if not first:
                        b_epilogue(b - 1, p)

            b_turn_x(0, True)
            b_project_qk(0, 0)
            b_project_v(0, 0, True)
            b_norms(0, 0, True, False)
            b_project_qk(0, 1)
            pe.wait_ge(b_v, 1)
            b_project_v(0, 1, True)
            b_batch(0, True, False)
            with pe.Fori(1, NB - 1) as b:
                b_batch(b, False, False)
            b_batch(NB - 1, False, True)
            b_turn_probs(NB - 1, NP - 1, 0, False)
            b_values(NB - 1, NP - 2, False)
            b_turn_probs(NB - 1, NP - 1, 1, False)
            b_values(NB - 1, NP - 1, False)
            for step in range(NP):
                b_epilogue(NB - 1, step)

            pe.wait_ge(s_wc, 32)
            pe.wait_ge(b_res, NB + 1)
            pe.wait_ge(b_glog, NB + 1)
            pe.wait_ge(b_exp, NB * H2)

            def c_up(ch, e):
                for c in range(FC):
                    if e >= 1:
                        pe.wait_ge(c_hid, ch * (NE * FC) + ((e - 1) * FC + c + 1))
                    nc.tensor.matmul(HB[c][:, :], w1_sb[:, e, c * P:(c + 1) * P], hTres[:, ds(ch * CW, CW)],
                                     start=True, stop=True).then_inc(c_h, 1)

            def c_down(ch, e):
                pe.wait_ge(c_hid, ch * (NE * FC) + (e + 1) * FC)
                if e >= 2:
                    pe.wait_ge(c_acc, ch * NE + e)
                else:
                    pe.wait_ge(c_acc, ch * NE + 1)
                for i in range(CT):
                    for c in range(FC):
                        last = nc.tensor.matmul(EB[e % 2][:, i * P:(i + 1) * P], hid[:, e % 2, c, i * P:(i + 1) * P],
                                                w2_sb[:, e * FC + c, :], start=(c == 0), stop=(c == FC - 1))
                last.then_inc(c_e, 1)

            with pe.Fori(0, NCH) as ch:
                for e in range(NE + 1):
                    if e < NE:
                        c_up(ch, e)
                    if e >= 1:
                        c_down(ch, e - 1)
                    if e == 3:
                        pe.wait_ge(c_g, ch + 1)
                        for i in range(CT):
                            last = nc.tensor.transpose(GT[0:NE, i * P:(i + 1) * P], gch[:, i, :], ident[:, :])
                        last.then_inc(c_gT_ps, 1)
                    if e == 5:
                        pe.wait_ge(c_gT, ch + 1)
                        for i in range(CT):
                            last = nc.tensor.matmul(GB[:, i * P:(i + 1) * P], gT[:, i * P:(i + 1) * P], b2_sb[:, :],
                                                    start=True, stop=True)
                        last.then_inc(c_gb, 1)

        @block.scalar
        def _(act):
            nc.scalar.preload_act_table_set("natural_log_exp_and_others")
            def a_load_x(b):
                act.wait_ge(a_xT_ps, b + 1)
                nc.scalar.copy(xT[:, :], VX[:, S:2 * S]).then_inc(a_xT, 1)

            def a_high_parts(n, start):
                act.wait_ge(a_qk_ps, n + 1)
                if not start:
                    act.wait_ge(a_scr, n * 16)
                nc.scalar.copy(parts[:, 0, :], QK[:, :]).then_inc(a_hi, 1)

            def a_rsqrt(which, n):
                act.wait_ge(a_mv[which], n)
                r = rstd3[:, which, :]
                nc.scalar.activation(r, mv3[:, which, :, 1], ACT.Ln, bias=epsln[:, :], scale=1.0).then_inc(a_lnv[which], 1)
                act.wait_ge(a_lnv[which], n)
                nc.scalar.activation(r, r, ACT.Exp, scale=-0.5).then_inc(a_rstd[which], 1)

            def a_group_output(n):
                act.wait_ge(a_pv, n)
                nc.scalar.copy(og[:, :], OG).then_inc(a_og, 1)

            def a_epilogue(b, k):
                if k == 9:
                    act.wait_ge(a_oT_ps, b + 1)
                    nc.scalar.copy(oT[:, :], YT).then_inc(a_oT, 1)
                if k == 11:
                    a_rsqrt(2, b + 1)

            def a_turned(b, h):
                act.wait_ge(a_t, b * H1 + (h + 1))
                nc.scalar.copy(probT[:, h % (2 * GH), :, :], TB[1][:, :].rearrange("p (j s) -> p j s", j=ST)
                               ).then_inc(a_pTs, 1)

            def a_batch(b, first, ahead):
                for k in range(H1):
                    if not first:
                        a_epilogue(b - 1, k)
                    if k % GH == 1 and (k > 5 or not first):
                        a_group_output(b * NG + (k // GH - 1))
                    if ahead and k == 6:
                        a_rsqrt(0, b + 3)
                    if ahead and k == 11:
                        a_load_x(b + 2)
                    if ahead and k == 15:
                        a_high_parts(b + 2, False)
                    if k % 2 == 0 and (k > 2 or not first):
                        a_turned(*((b, k - 3) if k >= 3 else (b - 1, k - 3 + H1)))
                    act.wait_ge(a_nmax, b * H1 + (k + 1))
                    if k >= 4 or not first:
                        act.wait_ge(a_t, b * H1 + (k - 3))
                    for i in range(ST):
                        last = nc.scalar.activation(prob[:, k % 4, i, :], SB[k % 3][:, i * S:(i + 1) * S], ACT.Exp,
                                                    bias=nmax[:, k % 4, i:i + 1], scale=1.0)
                    last.then_inc(a_exp, 1)

            act.wait_ge(s_const, 6)
            a_rsqrt(0, 1)
            a_load_x(0)
            a_high_parts(0, True)
            a_rsqrt(0, 2)
            act.wait_ge(a_v_ps, 1)
            a_load_x(1)
            a_high_parts(1, False)
            a_batch(0, True, True)
            with act.Fori(1, NB - 2) as b:
                a_batch(b, False, True)
            a_batch(NB - 2, False, False)
            a_batch(NB - 1, False, False)
            for k in range(12):
                if k in (0, 2):
                    a_turned(NB - 1, H1 - 3 + k)
                if k == 1:
                    a_group_output(NB * NG - 1)
                if k == 5:
                    a_group_output(NB * NG)
                a_epilogue(NB - 1, k)

            def b_turned_x(b):
                act.wait_ge(b_hT_ps, b + 1)
                nc.scalar.activation(hT[:, :], N2[:, 0:S], ACT.Identity, bias=vcols[:, R_B:R_B + 1],
                                     scale=vcols[:, R_G:R_G + 1]).then_inc(b_hT, 1)

            def b_out(b, p, first):
                if p == 0 and not first:
                    act.wait_ge(b_y, b)
                act.wait_ge(b_pv, b * NP + (p + 1))
                nc.scalar.copy(oT2[:, p, :], OV2[:, 0:S]).then_inc(b_oT, 1)

            def b_squares(b, p):
                act.wait_ge(b_qk_ps, b * NP + (p + 1))
                nc.scalar.activation(sq[:, :, :], QK2[p % 2][:, :].rearrange("p (a s) -> p a s", a=2), ACT.Square).then_inc(b_sq, 1)

            def b_load_v(b, p):
                act.wait_ge(b_v_ps, b * NP + (p + 1))
                nc.scalar.copy(vpair[:, p % 8, :, :], OV2[:, S:2 * S].rearrange("p (j d) -> p j d", j=ST)).then_inc(b_v, 1)

            def b_norms(b, p):
                act.wait_ge(b_n_ps, b * NP + (p + 1))
                norm = rr[:, p % 2, :, :].rearrange("p a s -> p (a s)")
                nc.scalar.activation(norm, N2[:, :], ACT.Ln, bias=eps12[:, :], scale=1.0).then_inc(b_ln, 1)
                act.wait_ge(b_ln, b * NP + (p + 1))
                nc.scalar.activation(norm, norm, ACT.Exp, scale=-0.5).then_inc(b_rr, 1)

            def b_exp_head(b, p, t):
                h = 2 * p + t
                act.wait_ge(b_m, b * H2 + (h + 1))
                nc.scalar.activation(prob2[:, h % 4, 0:P], smask[:, h % 4, 0:P], ACT.Exp,
                                     bias=nmax2[:, h % 4, 0:1], scale=-1.0, accum_out=sums[:, p % 2, t, 0:1])
                nc.scalar.activation(prob2[:, h % 4, P:3 * P], smask[:, h % 4, P:3 * P], ACT.Exp,
                                     bias=nmax2[:, h % 4, 1:2], scale=-1.0, accum_out=sums[:, p % 2, t, 1:2]
                                     ).then_inc(b_exp, 1)

            def b_rsqrt(which, n):
                act.wait_ge(b_mv[which], n)
                r = rstd3[:, which, :]
                nc.scalar.activation(r, mv3[:, which, :, 1], ACT.Ln, bias=epsln[:, :], scale=1.0).then_inc(b_lnv[which], 1)
                act.wait_ge(b_lnv[which], n)
                nc.scalar.activation(r, r, ACT.Exp, scale=-0.5).then_inc(b_rstd[which], 1)

            def b_epilogue_early(b, step):
                if step == 5:
                    act.wait_ge(b_h2T_ps, b + 1)
                    act.wait_ge(b_res, b + 1)
                    nc.scalar.activation(h2T[:, :], Y2[:, 0:S], ACT.Identity, bias=vcols[:, R_B:R_B + 1],
                                         scale=vcols[:, R_G:R_G + 1]).then_inc(b_h2T, 1)

            def b_epilogue_mid(b, step):
                if step == 3:
                    b_rsqrt(2, b + 1)
                if step == 6:
                    act.wait_ge(b_glog, b + 2)
                    nc.scalar.activation(gnorm[:, :, :], glog[:, :, :], ACT.Exp).then_inc(b_gexp, 1)

            def b_batch(b, first, last_batch):
                for p in range(NP):
                    more = p < NP - 1 or not last_batch
                    nb, np_ = (b, p + 1) if p < NP - 1 else (b + 1, 0)
                    ahead = p < NP - 2 or not last_batch
                    ab, ap = (b, p + 2) if p < NP - 2 else (b + 1, p + 2 - NP)
                    if not first or p >= 3:
                        b_out(*((b, p - 3) if p >= 3 else (b - 1, p - 3 + NP)), first)
                    if more:
                        b_norms(nb, np_)
                    if not first:
                        b_epilogue_early(b - 1, p)
                    b_exp_head(b, p, 0)
                    if ahead:
                        b_load_v(ab, ap)
                    if not first:
                        b_epilogue_mid(b - 1, p)
                    if p in (0, 2) and not last_batch:
                        b_rsqrt(p // 2, b + 2)
                    if ahead:
                        b_squares(ab, ap)
                    b_exp_head(b, p, 1)
                    if p == NP - 3 and not last_batch:
                        b_turned_x(b + 1)

            act.wait_ge(s_nat, 1)
            b_rsqrt(0, 1)
            b_rsqrt(1, 1)
            b_turned_x(0)
            b_squares(0, 0)
            b_load_v(0, 0)
            b_norms(0, 0)
            b_squares(0, 1)
            b_load_v(0, 1)
            b_batch(0, True, False)
            with act.Fori(1, NB - 1) as b:
                b_batch(b, False, False)
            b_batch(NB - 1, False, True)
            for p in range(NP - 3, NP):
                b_out(NB - 1, p, False)
            for step in range(NP):
                b_epilogue_early(NB - 1, step)
                b_epilogue_mid(NB - 1, step)

            nc.scalar.preload_act_table_set("gelu_apprx_tanh_and_others")
            with act.Fori(0, NCH) as ch:
                for e in range(NE):
                    if e == 4:
                        act.wait_ge(c_gT_ps, ch + 1)
                        nc.scalar.copy(gT[0:NE, :], GT[0:NE, :]).then_inc(c_gT, 1)
                    for c in range(FC):
                        act.wait_ge(c_h, ch * (NE * FC) + (e * FC + c + 1))
                        if c == 0:
                            act.wait_ge(c_e, ch * NE + max(e, 1))
                        nc.scalar.activation(hid[:, e % 2, c, :], HB[c][:, :], ACT.Gelu_apprx_tanh,
                                             bias=vcols[:, R_B1 + e * FC + c:R_B1 + e * FC + c + 1],
                                             scale=1.0).then_inc(c_hid, 1)

        @block.vector
        def _(dve):
            link0 = Link(dve, s_link, 0)
            for credit in (a_ydone, b_glog, c_acc, c_fin):
                dve.sem_inc(credit, 1)
            link0(nc.vector.memset(vaug[:, :, :, :], 0.0))
            nc.vector.memset(vaug[:, :, :, D1:D1 + 1], 1.0)
            link0(nc.vector.memset(blockones[:, :], 0.0))
            nc.vector.memset(blockones[0:D2, 0:D2], 1.0).then_inc(s_const, 1)
            nc.vector.memset(blockones[D2:P, D2:P], 1.0).then_inc(s_const, 1)
            def x_tile(b, i):
                return xres[:, ds((b * ST + i) * P, P)]

            def stats(which, tiles, link, mv_sem):
                for i, tile in enumerate(tiles):
                    last = nc.vector.bn_stats(bst3[:, which, i, :], tile)
                link(last)
                carry_wait()
                for i in range(ST):
                    last = nc.vector.bn_aggr(mv3[:, which, i, :], bst3[:, which, i, :])
                last.then_inc(mv_sem[which], 1)

            def norm(which, n, dst, src, rstd_sem):
                dve.wait_ge(rstd_sem[which], n)
                for i in range(ST):
                    last = nc.vector.tensor_scalar(dst[i], src[i], mv3[:, which, i, 0:1], rstd3[:, which, i:i + 1],
                                                   ALU.subtract, ALU.mult)
                return last

            xt = [tmp[:, i, :] for i in range(ST)]
            y_tiles = [Y1[:, i * P:(i + 1) * P] for i in range(ST)]

            def a_norm_x(b, step, link):
                if step == 0:
                    stats(0, [x_tile(b, i) for i in range(ST)], link, a_mv)
                else:
                    norm(0, b + 1, [xh[:, i, :] for i in range(ST)], [x_tile(b, i) for i in range(ST)], a_rstd
                         ).then_inc(a_xh, 1)

            def a_values(b, first):
                dve.wait_ge(a_v_ps, b + 1)
                if not first:
                    dve.wait_ge(a_pv, b * NG)
                nc.vector.tensor_copy(vaug[:, :, :, 0:D1], VX[:, 0:S].rearrange("p (i h d) -> p i h d", i=ST, h=H1)
                                      ).then_inc(a_v, 1)

            def a_rest_of(n, start):
                dve.wait_ge(a_hi, n + 1)
                if not start or n > 0:
                    dve.wait_ge(a_parts, n)
                nc.vector.tensor_tensor(rest[:, :], QK[:, :], parts[:, 0, :], ALU.subtract).then_inc(a_rest, 1)

            def a_turned(b, h):
                dve.wait_ge(a_t, b * H1 + (h + 1))
                nc.vector.tensor_copy(probT[:, h % (2 * GH), :, :], TB[0][:, :].rearrange("p (j s) -> p j s", j=ST)
                                      ).then_inc(a_pT, 1)

            def a_divide(b, g, link):
                dve.wait_ge(a_on_ps, b * NG + (g + 1))
                o = ON.rearrange("p (i t c) -> p i t c", i=ST, t=GH)
                link(nc.vector.reciprocal(rsum[:, :, :], o[:, :, :, D1]))
                dst = onat[:, :, g * GH * D1:(g + 1) * GH * D1].rearrange("p i (t d) -> p i t d", t=GH)
                nc.vector.tensor_tensor(dst, o[:, :, :, 0:D1], rsum[:, :, :].unsqueeze(3).broadcast_to([P, ST, GH, D1]),
                                        ALU.mult).then_inc(a_onat, 1)

            def a_epilogue(b, k, link):
                if k == 10:
                    dve.wait_ge(a_y, b + 1)
                    stats(2, y_tiles, link, a_mv)
                if k == 13:
                    link(norm(2, b + 1, xt, y_tiles, a_rstd))
                    for i in range(ST):
                        last = nc.vector.tensor_tensor(x_tile(b, i), x_tile(b, i), xt[i], ALU.add)
                    last.then_inc(a_ydone, 1)

            def a_batch(b, link, first, ahead):
                for k in range(H1):
                    if k % GH == 3 and (k > 7 or not first):
                        a_divide(*((b, k // GH - 2) if k > 7 else (b - 1, k // GH - 2 + NG)), link)
                    dve.wait_ge(a_s, b * H1 + (k + 1))
                    nc.vector.tensor_reduce(nmax[:, k % 4, :], SB[k % 3][:, :].rearrange("p (i t) -> p i t", i=ST),
                                            X_AXIS, ALU.max, negate=True).then_inc(a_nmax, 1)
                    if k % 2 == 1 and (k >= 3 or not first):
                        a_turned(*((b, k - 3) if k >= 3 else (b - 1, k - 3 + H1)))
                    if k == 5:
                        a_values(b, first)
                    if not first:
                        a_epilogue(b - 1, k, link)
                    if ahead and k in (5, 8):
                        a_norm_x(b + 2, 0 if k == 5 else 1, link)
                    if ahead and k == 15:
                        a_rest_of(b + 2, False)

            dve.wait_ge(s_x0, 16)
            dve.wait_ge(s_wa, 32)
            nc.vector.tensor_scalar_mul(wqkv_sb[:, 0:E], wqkv_sb[:, 0:E], float(D1) ** -0.5).then_inc(a_xh, 1)
            for n in range(2):
                a_norm_x(n, 0, link0)
                if n == 1:
                    dve.wait_ge(a_xT_ps, 1)
                a_norm_x(n, 1, link0)
                a_rest_of(n, True)
            link0(nc.vector.memset(kpair[:, :, :, :], 0.0))
            dve.wait_ge(s_vcol_ps, 1)
            link0(nc.vector.tensor_copy(vcols[:, :], bank[0][:, 0:P]))
            nc.vector.scalar_tensor_tensor(qks[:, :], vcols[:, R_QS:R_QS + NP], QK_SCALE, vcols[:, R_KS:R_KS + NP],
                                           ALU.mult, ALU.mult)
            for i, r in enumerate((R_G, R_B, R_GB)):
                last = nc.vector.tensor_copy(gspread[:, i, :], vcols[:, r:r + 1].broadcast_to([P, P]))
            last.then_inc(s_spread, 1)
            dve.wait_ge(s_nat_ps, 1)
            nc.vector.tensor_copy(gnat[:, :, :], bank[1][:, 0:2 * P].rearrange("p (a d) -> p a d", a=2))
            link0(nc.vector.tensor_copy(gbnat[:, :], bank[1][:, 2 * P:2 * P + NE]))
            nc.vector.tensor_copy(gbnat[:, 0:1], gbnat[:, 0:1]).then_inc(s_nat, 1)

            dve.wait_ge(s_x, 16 * (XQ - 1))
            link = Link(dve, a_link, 0)
            a_batch(0, link, True, True)
            n_a0 = link.n
            A_LINKS = 1 + NG + 2
            with dve.Fori(1, NB - 2) as b:
                link = Link(dve, a_link, (b - 1) * A_LINKS + n_a0)
                a_batch(b, link, False, True)
                assert link.n == A_LINKS, link.n
            link = Link(dve, a_link, (NB - 3) * A_LINKS + n_a0)
            a_batch(NB - 2, link, False, False)
            a_batch(NB - 1, link, False, False)
            for k in range(14):
                if k == 1:
                    a_turned(NB - 1, H1 - 2)
                if k in (3, 7):
                    a_divide(NB - 1, NG - 2 + k // GH, link)
                a_epilogue(NB - 1, k, link)
            dve.wait_ge(a_ydone, NB + 1)

            def b_stats(which, tiles, link):
                stats(which, tiles, link, b_mv)

            def b_norm(which, n, dst, src):
                return norm(which, n, dst, src, b_rstd)

            def b_norm_x(b, step, link):
                if step == 0:
                    b_stats(0, [x_tile(b, i) for i in range(ST)], link)
                if step == 1:
                    link(b_norm(0, b + 1, xt, [x_tile(b, i) for i in range(ST)]))
                if step == 2:
                    b_stats(1, xt, link)
                if step == 3:
                    b_norm(1, b + 1, [xh[:, i, :] for i in range(ST)], xt).then_inc(b_xh, 1)

            def b_normalize_qk(b, p):
                dve.wait_ge(b_rr, b * NP + (p + 1))
                nc.vector.scalar_tensor_tensor(qTs[:, p % 2, :], QK2[p % 2][:, 0:S], qks[:, p:p + 1], rr[:, p % 2, 0, :],
                                               ALU.mult, ALU.mult)
                for t in range(2):
                    r = slice(t * D2, (t + 1) * D2)
                    last = nc.vector.tensor_tensor(kpair[r, p % 2, t, :], QK2[p % 2][r, S:2 * S], rr[r, p % 2, 1, :], ALU.mult)
                last.then_inc(b_k, 1)

            def b_maxes(b, p, t):
                h = 2 * p + t
                dve.wait_ge(b_s, b * H2 + (h + 1))
                carry_wait()
                nc.vector.tensor_tensor_reduce(
                    out=smask[:, h % 4, 0:P], in0=S2[t][:, 0:P], in1=causal[:, 1, :],
                    scale=-1.0, scalar=3.0e38, op0=ALU.add, op1=ALU.min, accum_out=nmax2[:, h % 4, 0:1])
                nc.vector.tensor_tensor_reduce(
                    out=smask[:, h % 4, P:3 * P], in0=S2[t][:, P:3 * P], in1=causal[:, :, :].rearrange("p a s -> p (a s)"),
                    scale=-1.0, scalar=3.0e38, op0=ALU.add, op1=ALU.min, accum_out=nmax2[:, h % 4, 1:2]).then_inc(b_m, 1)

            def b_sums(b, p, t):
                dve.wait_ge(b_exp, b * H2 + (2 * p + t + 1))
                nc.vector.reciprocal(rblk[:, p % 2, t, 0:2], sums[:, p % 2, t, :])
                nc.vector.reciprocal(rblk[:, p % 2, t, 2:3], sums[:, p % 2, t, 1:2]).then_inc(b_rec, 1)

            def b_turned(b, p, t):
                dve.wait_ge(b_t, b * H2 + (2 * p + t + 1))
                nc.vector.tensor_copy(prob2T[:, p % 2, t, :], T2[:, 0:3 * P]).then_inc(b_pT, 1)

            def b_epilogue_early(b, step, link):
                if step == 3:
                    dve.wait_ge(b_y, b + 1)
                    b_stats(2, [Y2[:, i * P:(i + 1) * P] for i in range(ST)], link)
                if step == 6:
                    dve.wait_ge(b_gl, b + 1)
                    link(nc.vector.tensor_tensor(glog[:, :, :], Y2[:, 0:ST * NE].rearrange("p (i e) -> p i e", i=ST),
                                                 gbnat[:, :].unsqueeze(1).broadcast_to([P, ST, NE]), ALU.add))
                    link(nc.vector.tensor_reduce(gmx[:, :], glog[:, :, :], X_AXIS, ALU.max))
                    nc.vector.tensor_tensor(glog[:, :, :], glog[:, :, :],
                                            gmx[:, :].unsqueeze(2).broadcast_to([P, ST, NE]), ALU.subtract).then_inc(b_glog, 1)

            def b_epilogue_late(b, step, link):
                if step == 3:
                    b_norm(2, b + 1, [h2n[:, i, :] for i in range(ST)], [Y2[:, i * P:(i + 1) * P] for i in range(ST)]
                           ).then_inc(b_h2n, 1)
                if step == 6:
                    dve.wait_ge(b_gexp, b + 1)
                    link(nc.vector.tensor_reduce(gsm[:, :], gnorm[:, :, :], X_AXIS, ALU.add))
                    link(nc.vector.reciprocal(gmx[:, :], gsm[:, :]))
                    link(nc.vector.tensor_tensor(gnorm[:, :, :], gnorm[:, :, :],
                                                 gmx[:, :].unsqueeze(2).broadcast_to([P, ST, NE]), ALU.mult))
                    nc.vector.tensor_copy(gates[:, ds(b * (ST * NE), ST * NE)],
                                          gnorm[:, :, :].rearrange("p i e -> p (i e)")).then_inc(b_gate, 1)

            def b_batch(b, link, first, last_batch):
                for p in range(NP):
                    more = p < NP - 1 or not last_batch
                    nb, np_ = (b, p + 1) if p < NP - 1 else (b + 1, 0)
                    pb, pp = (b, p - 1) if p >= 1 else (b - 1, NP - 1)
                    if not first:
                        b_epilogue_early(b - 1, p, link)
                    if p in (0, 2) and not last_batch:
                        b_norm_x(b + 1, p, link)
                    b_maxes(b, p, 0)
                    if not first or p >= 1:
                        b_sums(pb, pp, 1)
                    if not first or p >= 1:
                        b_turned(pb, pp, 0)
                    if more:
                        b_normalize_qk(nb, np_)
                    b_maxes(b, p, 1)
                    b_sums(b, p, 0)
                    if not first or p >= 1:
                        b_turned(pb, pp, 1)
                    if not first:
                        b_epilogue_late(b - 1, p, link)
                    if p in (1, 3) and not last_batch:
                        b_norm_x(b + 1, 1 if p == 1 else 3, link)

            for step in range(4):
                b_norm_x(0, step, link0)
            b_normalize_qk(0, 0)
            n_first = 3
            B_LINKS = n_first + 1 + 5
            link = Link(dve, b_link, 0)
            b_batch(0, link, True, False)
            assert link.n == n_first, link.n
            with dve.Fori(1, NB - 1) as b:
                link = Link(dve, b_link, (b - 1) * B_LINKS + n_first)
                b_batch(b, link, False, False)
                assert link.n == B_LINKS, (link.n, B_LINKS)
            link = Link(dve, b_link, (NB - 2) * B_LINKS + n_first)
            b_batch(NB - 1, link, False, True)
            b_sums(NB - 1, NP - 1, 1)
            b_turned(NB - 1, NP - 1, 0)
            b_turned(NB - 1, NP - 1, 1)
            for step in range(NP):
                b_epilogue_early(NB - 1, step, link)
                b_epilogue_late(NB - 1, step, link)

            dve.wait_ge(b_gate, NB)

            def c_chunk(ch, half, link):
                dve.wait_ge(c_fin, ch + 1)
                nc.vector.tensor_copy(gch[:, :, :], gates[:, ds(ch * (CT * NE), CT * NE)].rearrange("p (i e) -> p i e", i=CT)
                                      ).then_inc(c_g, 1)
                dve.wait_ge(c_g, ch + 1)
                for e in range(NE):
                    dve.wait_ge(c_e, ch * NE + (e + 2))
                    for i in range(CT):
                        if e == 0:
                            last = nc.vector.tensor_scalar_mul(acc[:, i, :], EB[0][:, i * P:(i + 1) * P], gch[:, i, 0:1])
                        else:
                            last = nc.vector.scalar_tensor_tensor(acc[:, i, :], EB[e % 2][:, i * P:(i + 1) * P],
                                                                  gch[:, i, e:e + 1], acc[:, i, :], ALU.mult, ALU.add)
                    last.then_inc(c_acc, 1)
                    dve.wait_ge(c_acc, ch * NE + (e + 2))
                    if e == 5:
                        dve.wait_ge(c_gb, ch + 1)
                        link(nc.vector.tensor_tensor(acc[:, :, :], acc[:, :, :],
                                                     GB[:, :].rearrange("p (i d) -> p i d", i=CT), ALU.add))
                norm_stats(link, [acc[:, i, :] for i in range(CT)])
                for i in range(CT):
                    last = normalize(tmp[:, i, :], acc[:, i, :], i)
                link(last)
                link(nc.vector.tensor_tensor(acc[:, :, :], tmp[:, :, :],
                                             gnat[:, 0:1, :].broadcast_to([P, CT, P]), ALU.mult))
                link(nc.vector.tensor_tensor(tmp[:, :, :], acc[:, :, :],
                                             gnat[:, 1:2, :].broadcast_to([P, CT, P]), ALU.add))
                norm_stats(link, [tmp[:, i, :] for i in range(CT)])
                for i in range(CT):
                    last = normalize(acc[:, i, :], tmp[:, i, :], i)
                link(last)
                return nc.vector.tensor_tensor(fin[:, half, :, :], acc[:, :, :],
                                               xres[:, ds(ch * CW, CW)].rearrange("p (i d) -> p i d", i=CT), ALU.add)

            C_LINKS = 2 * NORM_LINKS + 5
            with dve.Fori(0, NCH // 2) as ii:
                link = Link(dve, c_link, ii * (2 * C_LINKS))
                for j in range(2):
                    if j == 0:
                        dve.wait_ge(s_out, ii * 32 + 16)
                    c_chunk(ii * 2 + j, j, link).then_inc(c_fin, 1)
                assert link.n == 2 * C_LINKS, link.n


_INS = ['L0_attn_x', 'L0_attn_w_qkv', 'L0_attn_w_out', 'L0_ffn_ln_g', 'L0_ffn_ln_b', 'L0_ffn_Wq', 'L0_ffn_Wk', 'L0_ffn_Wv',
        'L0_ffn_q_scale', 'L0_ffn_k_scale', 'L0_ffn_Wo', 'L0_ffn_gate_w', 'L0_ffn_gate_b', 'L0_ffn_w1', 'L0_ffn_b1',
        'L0_ffn_w2', 'L0_ffn_b2']


def kernel(**inputs):
    import numpy as _np
    import concourse.bacc as _bacc
    from concourse import mybir as _mybir
    from concourse.bass_utils import run_bass_kernel_spmd as _run

    nc = _bacc.Bacc("TRN2", target_bir_lowering=False, num_devices=1)
    arrays, args = {}, []
    for name in _INS:
        a = _np.ascontiguousarray(inputs[name])
        arrays[f"in_{name}"] = a
        args.append(nc.dram_tensor(f"in_{name}", a.shape, _mybir.dt.from_np(a.dtype), kind="ExternalInput").ap())
    shape = inputs['L0_attn_x'].shape
    args.append(nc.dram_tensor("out_0", shape, _mybir.dt.float32, kind="ExternalOutput").ap())
    sandwich_kernel(nc, *args)
    r = _run(nc, [arrays], core_ids=[0])
    return r.results[0]["out_0"]
```
